# Optimizing a Trainium2 kernel written in Bass

```python
import numpy as np
import jax
import jax.numpy as jnp

def _softmax(x, axis=-1):
    return jax.nn.softmax(x, axis=axis)

def _gelu(x):
    return jax.nn.gelu(x, approximate=True)

def _silu(x):
    return jax.nn.silu(x)

def _sigmoid(x):
    return jax.nn.sigmoid(x)

def _layernorm(x, axis=-1, eps=1e-05):
    m = jnp.mean(x, axis=axis, keepdims=True)
    v = jnp.var(x, axis=axis, keepdims=True)
    return (x - m) / jnp.sqrt(v + eps)

def _scatter_add(tgt, idx, src, axis=0):
    return tgt.at[idx].add(src)

def _segment_sum(src, seg, n):
    return jax.ops.segment_sum(src, seg, n)
kernel_name = 'mk_gnn_preln_d1_gnn_r8_d2d58e'

def setup_inputs(seed: int=0):
    np.random.seed(seed)
    _w = jnp.asarray

    def _rec_inputs():
        import jax
        import jax.numpy as jnp
        _gk = jax.random.key(seed)
        x = -0.000202 + 1 * jax.random.normal(jax.random.fold_in(_gk, 1), (12500, 128), jnp.float32)
        src = jax.random.randint(jax.random.fold_in(_gk, 2), (200000,), 0, 12500, jnp.int32)
        dst = jax.random.randint(jax.random.fold_in(_gk, 3), (200000,), 0, 12500, jnp.int32)
        _o = jnp.argsort(dst, stable=True)
        src = src[_o]
        dst = dst[_o]
        edge_attr_128 = 0.000133148 + 1.00009 * jax.random.normal(jax.random.fold_in(_gk, 12), (200000, 128), jnp.float32)
        return (x, src, dst, edge_attr_128)
    x, src, dst, edge_attr_128 = _rec_inputs()

    def _L0_gnn_setup():
        import jax, jax.numpy as jnp
        import numpy as np
        N_NODES = 6250
        N_EDGES = 100000
        H = 128
        LN_EPS = 1e-05

        def _layernorm(h, gamma, beta):
            mu = jnp.mean(h, axis=-1, keepdims=True)
            var = jnp.mean(jnp.square(h - mu), axis=-1, keepdims=True)
            return gamma * (h - mu) * jax.lax.rsqrt(var + LN_EPS) + beta
        key = jax.random.key(seed)
        ks = jax.random.split(key, 8)
        x = jax.random.normal(ks[0], (N_NODES, H), dtype=jnp.float32)
        senders = jax.random.randint(ks[1], (N_EDGES,), 0, N_NODES, dtype=jnp.int32)
        receivers = jax.random.randint(ks[2], (N_EDGES,), 0, N_NODES, dtype=jnp.int32)
        edge_feat = jax.random.normal(ks[3], (N_EDGES, H), dtype=jnp.float32)
        lim = 1.0 / np.sqrt(3 * H)
        W1 = jax.random.uniform(ks[4], (3 * H, H), minval=-lim, maxval=lim, dtype=jnp.float32)
        b1 = jax.random.uniform(ks[5], (H,), minval=-lim, maxval=lim, dtype=jnp.float32)
        ln_gamma = jnp.ones((H,), dtype=jnp.float32)
        ln_beta = jnp.zeros((H,), dtype=jnp.float32)
        return {'x': x, 'senders': senders, 'receivers': receivers, 'edge_feat': edge_feat, 'W1': W1, 'b1': b1, 'ln_gamma': ln_gamma, 'ln_beta': ln_beta}
    _L0_gnn_all = _L0_gnn_setup()
    _L0_gnn_in = {k: v for k, v in _L0_gnn_all.items() if k in ('W1', 'b1', 'ln_gamma', 'ln_beta')}
    del _L0_gnn_all
    return {'x': x, 'src': src, 'dst': dst, 'edge_attr_128': edge_attr_128, 'L0_gnn_W1': _L0_gnn_in['W1'], 'L0_gnn_b1': _L0_gnn_in['b1'], 'L0_gnn_ln_gamma': _L0_gnn_in['ln_gamma'], 'L0_gnn_ln_beta': _L0_gnn_in['ln_beta']}

def reference(x, src, dst, edge_attr_128, L0_gnn_W1, L0_gnn_b1, L0_gnn_ln_gamma, L0_gnn_ln_beta):
    import jax
    import jax.numpy as jnp

    def _L0_gnn_ref(x, senders, receivers, edge_feat, W1, b1, ln_gamma, ln_beta):
        import jax, jax.numpy as jnp
        import numpy as np
        N_NODES = 6250
        N_EDGES = 100000
        H = 128
        LN_EPS = 1e-05

        def _layernorm(h, gamma, beta):
            mu = jnp.mean(h, axis=-1, keepdims=True)
            var = jnp.mean(jnp.square(h - mu), axis=-1, keepdims=True)
            return gamma * (h - mu) * jax.lax.rsqrt(var + LN_EPS) + beta
        cat = jnp.concatenate((x[senders], x[receivers], edge_feat), axis=-1)
        msg = jax.nn.relu(cat @ W1 + b1)
        aggr = jax.ops.segment_sum(msg, receivers, num_segments=x.shape[0])
        h = aggr + x
        return _layernorm(h, ln_gamma, ln_beta)
    h = jnp.maximum(_layernorm(x, axis=-1), 0.0)
    x = x + _L0_gnn_ref(h, src, dst, edge_attr_128, L0_gnn_W1, L0_gnn_b1, L0_gnn_ln_gamma, L0_gnn_ln_beta)
    return x

_drawn_inputs = setup_inputs


def setup_inputs(seed=0):
    import zlib

    import numpy as np

    out = dict(_drawn_inputs(seed))
    spreads = {'L0_gnn_ln_gamma': (1.0, 0.2), 'L0_gnn_ln_beta': (0.0, 0.1)}
    factors = {}
    for name, (base, spread) in spreads.items():
        noise = np.random.default_rng([zlib.crc32(name.encode()), seed]).standard_normal(out[name].shape)
        drawn = base * np.exp(spread * noise) if base else spread * noise
        out[name] = jnp.asarray(drawn.astype(out[name].dtype))
    for name, factor in factors.items():
        out[name] = (out[name] * factor).astype(out[name].dtype)
    return out
```

```python
from contextlib import ExitStack

import concourse.bass as bass
from concourse import mybir

F32 = mybir.dt.float32
I32 = mybir.dt.int32
ALU = mybir.AluOpType
ACT = mybir.ActivationFunctionType
AX = mybir.AxisListType

P = 128
H = 128
EPS = 1e-5
SUB = 4
GROUP = P * SUB
UNROLL = 4
WIN = 64
LEAD = 128
WIDE = 512
CHUNK = 7


def build(nc, x, src, dst, edge_attr, w1, b1, gamma, beta, out):
    N, E = x.shape[0], edge_attr.shape[0]
    BLOCKS = -(-N // P)
    LAST_ROWS = N - (BLOCKS - 1) * P
    FULL_GROUPS = E // GROUP
    ROUNDS = -(-(-(-E // GROUP)) // UNROLL)
    GROUPS = ROUNDS * UNROLL
    TAIL_START = E - GROUP
    TAIL_DONE = (FULL_GROUPS * GROUP - TAIL_START) // SUB
    QUADS = 4
    ROWS = GROUPS // QUADS
    PER_BLOCK = P // (N * GROUP // E)
    CHUNKS = BLOCKS // CHUNK
    TABLE_ROWS = BLOCKS * P + P
    WIDES = -(-(BLOCKS * P) // WIDE)
    assert BLOCKS == ROUNDS and PER_BLOCK == UNROLL and CHUNKS % 2 == 0 and CHUNKS * CHUNK == BLOCKS
    assert E % SUB == 0 and FULL_GROUPS * GROUP < E and ROWS * QUADS == GROUPS and ROWS <= P

    table_a = nc.dram_tensor("table_a", (BLOCKS * P, H), F32)
    table_b = nc.dram_tensor("table_b", (TABLE_ROWS, H), F32)

    ctx = ExitStack()
    with ctx:
        def sb(name, shape, dt=F32):
            return ctx.enter_context(nc.sbuf_tensor(name, shape, dt))

        def bank(name):
            return ctx.enter_context(nc.psum_tensor(name, [P, 512], F32))

        def sem(name):
            return ctx.enter_context(nc.semaphore(name))

        x_all = sb("x_all", [P, BLOCKS, H])
        aggr = sb("aggr", [P, WIDES * WIDE])
        src_f = sb("src_f", [P, GROUPS, SUB])
        dst_f = sb("dst_f", [P, GROUPS, SUB])
        base_i = sb("base_i", [1, GROUPS], I32)
        scale_all = sb("scale_all", [P, BLOCKS])
        shift_all = sb("shift_all", [P, BLOCKS])
        ident = sb("ident", [P, P])
        ones = sb("ones", [P, P])
        count = sb("count", [P, WIDE])
        w_ab = sb("w_ab", [P, 2 * H])
        w_c = sb("w_c", [P, H])
        b1_all = sb("b1_all", [P, H])
        gamma_all = sb("gamma_all", [P, H])
        beta_all = sb("beta_all", [P, H])
        flag = sb("flag", [1, 1], I32)
        h_rows = sb("h_rows", [P, CHUNK, H])
        h_cols = sb("h_cols", [P, CHUNK, P])
        a_out = sb("a_out", [P, 2, CHUNK, H])
        b_out = sb("b_out", [P, 2, CHUNK, H])
        moments6 = sb("moments6", [P, CHUNK, 6])
        moments = sb("moments", [P, CHUNK, 2])
        deviation = sb("deviation", [P, CHUNK])
        ids_i = aggr[:, 0:2 * QUADS * GROUP].bitcast(I32).rearrange("p (a q e) -> p a q e", a=2, q=QUADS)
        ids_f = aggr[:, 2 * QUADS * GROUP:4 * QUADS * GROUP].rearrange("p (a q e) -> p a q e", a=2, q=QUADS)
        lowest = sb("lowest", [P, QUADS])
        highest = sb("highest", [P, QUADS])
        floor_of = sb("floor_of", [P, QUADS])
        bad = sb("bad", [P, QUADS])
        diagonal = sb("diagonal", [P, QUADS, P])
        edges = sb("edges", [P, UNROLL, GROUP])
        a_rows = sb("a_rows", [P, UNROLL, SUB, H])
        b_win = sb("b_win", [P, UNROLL, H])
        picks = sb("picks", [P, UNROLL, SUB], I32)
        onehot = sb("onehot", [P, 4, SUB, P])
        edge_cols = sb("edge_cols", [P, 2, GROUP])
        onehot_cols = sb("onehot_cols", [P, 2, GROUP])
        msg = sb("msg", [P, 2, SUB, H])
        staged = sb("staged", [P, P])
        h_again = sb("h_again", [P, H])
        total = sb("total", [P, H])
        out_rows = sb("out_rows", [P, H])
        o_moments6 = sb("o_moments6", [P, 6])
        o_moments = sb("o_moments", [P, 2])
        o_var = sb("o_var", [P, 1])
        o_dev = sb("o_dev", [P, 1])
        o_scale = sb("o_scale", [P, 1])

        ps_edge = [bank("ps_edge0"), bank("ps_edge1")]
        ps_hot = [bank("ps_hot0"), bank("ps_hot1")]
        ps_pre = [bank("ps_pre0"), bank("ps_pre1")]
        ps_sum = bank("ps_sum")
        ps_fin = bank("ps_fin")
        ps_sums = [ps_sum[:, 0:WIN], ps_fin[:, P:P + WIN]]
        ps_turn = [ps_edge[0], ps_edge[1]]
        ps_tab = [ps_hot[0], ps_hot[1], ps_pre[0], ps_pre[1]]

        s_weights = sem("s_weights")
        s_ids = sem("s_ids")
        s_x = [sem("s_x0"), sem("s_x1")]
        s_pad = sem("s_pad")
        s_const = sem("s_const")
        s_cast = sem("s_cast")
        s_range = sem("s_range")
        s_diag = sem("s_diag")
        s_ids_turned = sem("s_ids_turned")
        s_ids_kept = sem("s_ids_kept")
        s_plan = sem("s_plan")
        s_planned = sem("s_planned")
        s_vec = sem("s_vec")
        s_var = sem("s_var")
        s_dev = sem("s_dev")
        s_norm = sem("s_norm")
        s_h = sem("s_h")
        s_h_turned = sem("s_h_turned")
        s_h_cols = sem("s_h_cols")
        s_tab = sem("s_tab")
        s_a_kept = sem("s_a_kept")
        s_b_kept = sem("s_b_kept")
        s_a_stored = [sem("s_a_stored0"), sem("s_a_stored1")]
        s_b_stored = [sem("s_b_stored0"), sem("s_b_stored1")]
        s_zero = sem("s_zero")
        s_zero_row = sem("s_zero_row")
        s_gate_pool = sem("s_gate_pool")
        s_gate_dve = sem("s_gate_dve")
        s_edges = [sem(f"s_edges{u}") for u in range(UNROLL)]
        s_b_win = [sem(f"s_b_win{u}") for u in range(UNROLL)]
        s_a_rows = [[sem(f"s_a_rows{u}_{k}") for k in range(SUB)] for u in range(UNROLL)]
        s_picks = sem("s_picks")
        s_rel = sem("s_rel")
        s_hot = sem("s_hot")
        s_edge_turned = sem("s_edge_turned")
        s_hot_turned = sem("s_hot_turned")
        s_edge_cols = sem("s_edge_cols")
        s_hot_cols = sem("s_hot_cols")
        s_pre = sem("s_pre")
        s_z = sem("s_z")
        s_msg = sem("s_msg")
        s_sum = sem("s_sum")
        s_added = sem("s_added")
        s_staged = sem("s_staged")
        s_h_again = sem("s_h_again")
        s_fin_turned = sem("s_fin_turned")
        s_total = sem("s_total")
        s_o_vec = sem("s_o_vec")
        s_o_var = sem("s_o_var")
        s_o_dev = sem("s_o_dev")
        s_out = sem("s_out")
        s_out_stored = sem("s_out_stored")
        g_edges = sem("g_edges")
        g_picks = sem("g_picks")
        g_rows = [sem(f"g_rows{k}") for k in range(2 * SUB)]
        g_turned = sem("g_turned")
        g_cols = sem("g_cols")
        g_pre = sem("g_pre")
        g_z = sem("g_z")
        g_z2 = sem("g_z2")
        g_msg = sem("g_msg")
        g_hot = sem("g_hot")
        g_sum = sem("g_sum")
        g_added = sem("g_added")

        block = ctx.enter_context(nc.Block())

        def node_rows(tensor, c):
            return tensor[bass.ds(c * (CHUNK * P), CHUNK * P), :].rearrange("(b p) f -> p b f", p=P)

        def group_rows(start):
            return edge_attr[bass.ds(start, GROUP), :].rearrange("(p k) f -> p (k f)", p=P)

        def start_of(i, u):
            if isinstance(i, int) and i * UNROLL + u >= FULL_GROUPS:
                return TAIL_START
            return i * (UNROLL * GROUP) + u * GROUP

        @block.sync
        def _(sp):
            for a, ids in enumerate((src, dst)):
                full = FULL_GROUPS - (QUADS - 1) * ROWS
                sp.dma_start(ids_i[0:ROWS, a, 0:QUADS - 1, :],
                             ids[0:(QUADS - 1) * ROWS * GROUP].rearrange("(q r e) -> r q e", q=QUADS - 1, r=ROWS)
                             ).then_inc(s_ids, 16)
                sp.dma_start(ids_i[0:full, a, QUADS - 1, :],
                             ids[(QUADS - 1) * ROWS * GROUP:FULL_GROUPS * GROUP].rearrange("(r e) -> r e", r=full)
                             ).then_inc(s_ids, 16)
                for r in range(full, ROWS):
                    sp.dma_start(ids_i[r:r + 1, a, QUADS - 1, :],
                                 ids[TAIL_START:E].rearrange("(r e) -> r e", r=1)).then_inc(s_ids, 16)

            def load_x(c, u):
                if not isinstance(c, int) or c + u < CHUNKS - 1:
                    sp.dma_start(x_all[:, bass.ds((c + u) * CHUNK, CHUNK), :], node_rows(x, c + u)
                                 ).then_inc(s_x[u], 16)
                else:
                    first = (CHUNKS - 1) * CHUNK
                    sp.dma_start(x_all[:, first:BLOCKS - 1, :],
                                 x[first * P:(BLOCKS - 1) * P, :].rearrange("(b p) f -> p b f", p=P)
                                 ).then_inc(s_x[u], 16)
                    sp.wait_ge(s_pad, 1)
                    sp.dma_start(x_all[0:LAST_ROWS, BLOCKS - 1, :], x[(BLOCKS - 1) * P:N, :]
                                 ).then_inc(s_x[u], 16)

            load_x(0, 0)
            load_x(0, 1)
            sp.dma_start(w_ab[:, 0:H], w1[0:H, :]).then_inc(s_weights, 16)
            sp.dma_start(w_ab[:, H:2 * H], w1[H:2 * H, :]).then_inc(s_weights, 16)
            sp.dma_start(w_c[:, :], w1[2 * H:3 * H, :]).then_inc(s_weights, 16)
            for tile, row in ((b1_all, b1), (gamma_all, gamma), (beta_all, beta)):
                sp.dma_start(tile[:, :], row.rearrange("(o f) -> o f", o=1).to_broadcast([P, H])
                             ).then_inc(s_weights, 16)
            with sp.Fori(1, CHUNKS // 2 - 1) as c:
                for u in range(2):
                    sp.wait_ge(s_x[u], c * 16)
                    load_x(c * 2, u)
            for u in range(2):
                sp.wait_ge(s_x[u], (CHUNKS // 2 - 1) * 16)
                load_x(CHUNKS - 2, u)

            sp.wait_ge(s_zero_row, 1)
            sp.dma_start(table_b[BLOCKS * P:TABLE_ROWS, :], onehot[:, 0, 0, :]).then_inc(s_b_stored[0], 16)

            sp.wait_ge(s_planned, 3)
            crooked = sp.value_load(flag[0:1, 0:1], min_val=0, max_val=GROUPS)
            for u in range(2):
                sp.wait_ge(s_b_stored[u], (CHUNKS // 2) * 16 + (16 if u == 0 else 0))

            with sp.If(crooked < 1):
                def step(i, u):
                    later = not isinstance(i, int) or i > 0
                    if later:
                        sp.wait_ge(s_edge_turned, (i - 1) * UNROLL + u + 1)
                    sp.dma_start(edges[:, u, :], group_rows(start_of(i, u))).then_inc(s_edges[u], 16)
                    if later:
                        sp.wait_ge(s_pre, (i - 1) * UNROLL + u + 1)
                    base = sp.value_load(base_i[0:1, bass.ds(i * UNROLL + u, 1)], min_val=0, max_val=N - 1)
                    sp.dma_start(b_win[:, u, :], table_b[bass.ds(base, P), :]).then_inc(s_b_win[u], 16)

                for u in range(UNROLL):
                    step(0, u)
                for u in range(UNROLL):
                    step(1, u)
                for u in range(UNROLL):
                    step(2, u)
                with sp.Fori(3, ROUNDS - 1) as i:
                    for u in range(UNROLL):
                        step(i, u)
                    sp.wait_ge(s_out, i - 2)
                    sp.dma_start(out[bass.ds((i - 3) * P, P), :], out_rows[:, :]).then_inc(s_out_stored, 16)
                for u in range(UNROLL):
                    step(ROUNDS - 1, u)
                for b in range(ROUNDS - 4, BLOCKS):
                    rows = P if b < BLOCKS - 1 else LAST_ROWS
                    sp.wait_ge(s_out, b + 1)
                    sp.dma_start(out[b * P:b * P + rows, :], out_rows[0:rows, :]).then_inc(s_out_stored, 16)
                sp.wait_ge(s_out_stored, BLOCKS * 16)
            with sp.Else():
                def load(g, start):
                    sp.wait_ge(g_turned, g)
                    sp.dma_start(edges[:, 0, :], group_rows(start)).then_inc(g_edges, 16)

                with sp.Fori(0, FULL_GROUPS) as g:
                    load(g, g * GROUP)
                for g in range(FULL_GROUPS, GROUPS):
                    load(g, TAIL_START)
                with sp.Fori(0, BLOCKS - 1) as b:
                    sp.wait_ge(s_out, b + 1)
                    sp.dma_start(out[bass.ds(b * P, P), :], out_rows[:, :]).then_inc(s_out_stored, 16)
                sp.wait_ge(s_out, BLOCKS)
                sp.dma_start(out[(BLOCKS - 1) * P:N, :], out_rows[0:LAST_ROWS, :]).then_inc(s_out_stored, 16)
                sp.wait_ge(s_out_stored, BLOCKS * 16)

        @block.gpsimd
        def _(pool):
            pool.memset(x_all[:, BLOCKS - 1, :], 0.0).then_inc(s_pad, 1)
            pool.memset(ident[:, :], 0.0).then_inc(s_const, 1)
            pool.memset(ones[:, :], 1.0).then_inc(s_const, 1)
            pool.iota(count[:, :], pattern=[[1, WIDE]], base=0, channel_multiplier=0,
                      allow_small_or_imprecise_dtypes=True).then_inc(s_const, 1)
            pool.iota(floor_of[:, :], pattern=[[ROWS * P // PER_BLOCK, QUADS]], base=-LEAD,
                      channel_multiplier=P // PER_BLOCK,
                      allow_small_or_imprecise_dtypes=True).then_inc(s_const, 1)
            pool.wait_ge(s_const, 4)
            pool.affine_select(out=ident[:, :], in_=ident[:, :], compare_op=ALU.not_equal, fill=1.0,
                               base=0, pattern=[[-1, P]], channel_multiplier=1).then_inc(s_const, 1)
            pool.memset(onehot[:, :, :, :], 0.0).then_inc(s_zero_row, 1)
            pool.wait_ge(s_ids_turned, 4 * QUADS // 2)
            pool.wait_ge(s_range, 2)
            pool.memset(aggr[:, :], 0.0).then_inc(s_zero, 1)
            for u in range(2):
                pool.wait_ge(s_a_stored[u], (CHUNKS // 2) * 16)
            pool.wait_ge(s_planned, 3)
            crooked = pool.value_load(flag[0:1, 0:1], min_val=0, max_val=GROUPS)

            with pool.If(crooked < 1):
                def step(i, u):
                    pool.wait_ge(s_picks, i * UNROLL + u + 1)
                    if not isinstance(i, int) or i > 0:
                        pool.wait_ge(s_z, (i - 1) * UNROLL + u + 1)
                    pool.sem_inc(s_gate_pool, 1)
                    for k in range(SUB):
                        pool.indirect_dma_start(
                            a_rows[:, u, k, :], None, table_a[:, :],
                            bass.IndirectOffsetOnAxis(ap=picks[:, u, k:k + 1], axis=0),
                        ).then_inc(s_a_rows[u][k], 16)

                for u in range(UNROLL):
                    step(0, u)
                with pool.Fori(1, ROUNDS) as i:
                    for u in range(UNROLL):
                        step(i, u)
            with pool.Else():
                with pool.Fori(0, GROUPS) as g:
                    pool.wait_ge(g_picks, (g + 1) * 2)
                    pool.wait_ge(g_z2, g)
                    pool.sem_inc(s_gate_pool, 1)
                    for k in range(SUB):
                        pool.indirect_dma_start(
                            a_rows[:, 0, k, :], None, table_a[:, :],
                            bass.IndirectOffsetOnAxis(ap=picks[:, 0, k:k + 1], axis=0),
                        ).then_inc(g_rows[k], 16)
                        pool.indirect_dma_start(
                            a_rows[:, 1, k, :], None, table_b[:, :],
                            bass.IndirectOffsetOnAxis(ap=picks[:, 1, k:k + 1], axis=0),
                        ).then_inc(g_rows[SUB + k], 16)

        @block.tensor
        def _(pe):
            pe.wait_ge(s_const, 5)
            pe.wait_ge(s_cast, 1)
            n = 0
            for a in range(2):
                for q in range(QUADS):
                    if n >= 2:
                        pe.wait_ge(s_ids_kept, n - 1)
                    for k in range(SUB):
                        mm = pe.transpose(ps_turn[n % 2][:, k * ROWS:(k + 1) * ROWS],
                                          ids_f[0:ROWS, a, q, k::SUB], ident[0:ROWS, 0:ROWS])
                    mm.then_inc(s_ids_turned, 1)
                    n += 1
            pe.wait_ge(s_diag, 2)
            for q in range(QUADS):
                pe.matmul(ps_sum[:, q * ROWS:(q + 1) * ROWS], ones[0:ROWS, :], diagonal[0:ROWS, q, 0:ROWS],
                          start=True, stop=True)
            for q in range(QUADS):
                mm = pe.matmul(ps_fin[0:1, 0:1], bad[0:ROWS, q:q + 1], ones[0:ROWS, 0:1],
                               start=(q == 0), stop=(q == QUADS - 1))
            mm.then_inc(s_plan, 1)
            pe.wait_ge(s_weights, 96)
            pe.wait_ge(s_ids_kept, 2 * QUADS)

            def turn_h(c):
                pe.wait_ge(s_h, c + 1)
                if not isinstance(c, int) or c > 0:
                    pe.wait_ge(s_h_cols, c)
                for k in range(CHUNK):
                    mm = pe.transpose(ps_turn[k // 4][:, (k % 4) * P:(k % 4 + 1) * P], h_rows[:, k, :], ident[:, :])
                mm.then_inc(s_h_turned, 1)

            def tables(c):
                pe.wait_ge(s_h_cols, c + 1)
                if not isinstance(c, int) or c > 0:
                    pe.wait_ge(s_a_kept, c)
                    pe.wait_ge(s_b_kept, c)
                for k in range(CHUNK):
                    for t in range(2):
                        mm = pe.matmul(ps_tab[2 * t + k // 4][:, (k % 4) * H:(k % 4 + 1) * H],
                                       h_cols[:, k, :], w_ab[:, t * H:(t + 1) * H], start=True, stop=True)
                mm.then_inc(s_tab, 1)

            with pe.Fori(0, CHUNKS) as c:
                turn_h(c)
                tables(c)

            pe.wait_ge(s_planned, 3)
            crooked = pe.value_load(flag[0:1, 0:1], min_val=0, max_val=GROUPS)
            pe.wait_ge(s_a_kept, CHUNKS)
            pe.wait_ge(s_b_kept, CHUNKS)

            def turn_total(b):
                pe.wait_ge(s_staged, b + 1)
                if not isinstance(b, int) or b > 0:
                    pe.wait_ge(s_total, b)
                pe.transpose(ps_fin[:, 0:P], staged[:, :], ident[:, :]).then_inc(s_fin_turned, 1)

            with pe.If(crooked < 1):
                def turn(i, u):
                    g, later = i * UNROLL + u, not isinstance(i, int) or i * UNROLL + u >= 2
                    pe.wait_ge(s_edges[u], (i + 1) * 16)
                    if later:
                        pe.wait_ge(s_edge_cols, g - 1)
                    for k in range(SUB):
                        mm = pe.transpose(ps_edge[u % 2][:, k * P:(k + 1) * P],
                                          edges[:, u, k * H:(k + 1) * H], ident[:, :])
                    mm.then_inc(s_edge_turned, 1)
                    pe.wait_ge(s_hot, g + 1)
                    if later:
                        pe.wait_ge(s_hot_cols, g - 1)
                    for k in range(SUB):
                        mm = pe.transpose(ps_hot[u % 2][:, k * P:(k + 1) * P], onehot[:, u, k, :], ident[:, :])
                    mm.then_inc(s_hot_turned, 1)

                def products(i, u):
                    g, later = i * UNROLL + u, not isinstance(i, int) or i * UNROLL + u >= 2
                    pe.wait_ge(s_edge_cols, g + 1)
                    pe.wait_ge(s_hot_cols, g + 1)
                    pe.wait_ge(s_b_win[u], (i + 1) * 16)
                    if later:
                        pe.wait_ge(s_z, g - 1)
                    for k in range(SUB):
                        to = ps_pre[u % 2][:, k * H:(k + 1) * H]
                        pe.matmul(to, edge_cols[:, u % 2, k * P:(k + 1) * P], w_c[:, :], start=True, stop=False)
                        mm = pe.matmul(to, onehot_cols[:, u % 2, k * P:(k + 1) * P], b_win[:, u, :],
                                       start=False, stop=True)
                    mm.then_inc(s_pre, 1)

                def sums(i, u):
                    g, later = i * UNROLL + u, not isinstance(i, int) or i * UNROLL + u >= 2
                    pe.wait_ge(s_msg, g + 1)
                    if later:
                        pe.wait_ge(s_added, g - 1)
                    if u == 3 and not (isinstance(i, int) and i < 2):
                        pe.wait_ge(s_total, i - 1)
                    for k in range(SUB):
                        mm = pe.matmul(ps_sums[u % 2], msg[:, u % 2, k, :],
                                       onehot[:, u, k, 0:WIN], start=(k == 0), stop=(k == SUB - 1))
                    mm.then_inc(s_sum, 1)

                def round_(i, first=False, last=False, finish=True):
                    for u in range(UNROLL):
                        if not (last and u == UNROLL - 1):
                            turn(i if u < UNROLL - 1 else i + 1, (u + 1) % UNROLL)
                        products(i, u)
                        if u == 2 and finish:
                            turn_total(i - 2)
                        if not (first and u == 0):
                            sums(i if u else i - 1, (u - 1) % UNROLL)

                turn(0, 0)
                round_(0, first=True, finish=False)
                round_(1, finish=False)
                with pe.Fori(2, ROUNDS - 1) as i:
                    round_(i)
                round_(ROUNDS - 1, last=True)
                sums(ROUNDS - 1, UNROLL - 1)
                turn_total(BLOCKS - 2)
                turn_total(BLOCKS - 1)
            with pe.Else():
                with pe.Fori(0, GROUPS) as g:
                    pe.wait_ge(g_edges, (g + 1) * 16)
                    for k in range(SUB):
                        mm = pe.transpose(ps_edge[0][:, k * P:(k + 1) * P],
                                          edges[:, 0, k * H:(k + 1) * H], ident[:, :])
                    mm.then_inc(g_turned, 1)
                    pe.wait_ge(g_cols, g + 1)
                    pe.wait_ge(g_z, g)
                    for k in range(SUB):
                        mm = pe.matmul(ps_pre[0][:, k * H:(k + 1) * H], edge_cols[:, 0, k * P:(k + 1) * P],
                                       w_c[:, :], start=True, stop=True)
                    mm.then_inc(g_pre, 1)
                    with pe.Fori(0, WIDES) as w:
                        pe.wait_ge(g_msg, g + 1)
                        pe.wait_ge(g_hot, g * WIDES + w + 1)
                        pe.wait_ge(g_added, g * WIDES + w)
                        for k in range(SUB):
                            mm = pe.matmul(ps_sum[:, :], msg[:, 0, k, :], onehot[:, k, :, :],
                                           start=(k == 0), stop=(k == SUB - 1))
                        mm.then_inc(g_sum, 1)
                with pe.Fori(0, BLOCKS) as b:
                    pe.wait_ge(s_total, b)
                    turn_total(b)

        @block.scalar
        def _(act):
            n = 0
            for a, ids in enumerate((src_f, dst_f)):
                for q in range(QUADS):
                    act.wait_ge(s_ids_turned, n + 1)
                    act.activation(ids[:, q * ROWS:(q + 1) * ROWS, :].rearrange("p r k -> p k r"),
                                   ps_turn[n % 2][:, 0:SUB * ROWS].rearrange("p (k r) -> p k r", k=SUB),
                                   ACT.Copy).then_inc(s_ids_kept, 1)
                    n += 1

            with act.Fori(0, CHUNKS // 2) as pair:
                for par in range(2):
                    c = pair * 2 + par
                    act.wait_ge(s_var, c + 1)
                    act.activation(deviation[:, :], moments[:, :, 1], ACT.Sqrt).then_inc(s_dev, 1)
                    act.wait_ge(s_norm, c + 1)
                    act.wait_ge(s_h_turned, c)
                    for k in range(CHUNK):
                        b = c * CHUNK + k
                        ins = act.activation(h_rows[:, k, :], x_all[:, bass.ds(b, 1), :].rearrange("p o f -> p (o f)"),
                                             ACT.Relu, bias=shift_all[:, bass.ds(b, 1)],
                                             scale=scale_all[:, bass.ds(b, 1)])
                    ins.then_inc(s_h, 1)
                    act.wait_ge(s_h_turned, c + 1)
                    act.wait_ge(s_tab, c)
                    act.activation(h_cols[:, 0:4, :].rearrange("p b n -> p (b n)"), ps_turn[0][:, :], ACT.Copy)
                    act.activation(h_cols[:, 4:CHUNK, :].rearrange("p b n -> p (b n)"),
                                   ps_turn[1][:, 0:(CHUNK - 4) * P], ACT.Copy).then_inc(s_h_cols, 1)
                    act.wait_ge(s_tab, c + 1)
                    act.wait_ge(s_a_stored[par], pair * 16)
                    for m in range(2):
                        nb = min(4, CHUNK - 4 * m)
                        ins = act.activation(a_out[:, par, 4 * m:4 * m + nb, :].rearrange("p b f -> p (b f)"),
                                             ps_tab[m][:, 0:nb * H], ACT.Copy)
                    ins.then_inc(s_a_kept, 1)
                    act.wait_ge(s_a_kept, c + 1)
                    act.dma_start(node_rows(table_a, c), a_out[:, par, :, :]).then_inc(s_a_stored[par], 16)
                    act.wait_ge(s_b_kept, c + 1)
                    act.dma_start(node_rows(table_b, c), b_out[:, par, :, :]).then_inc(s_b_stored[par], 16)

            act.wait_ge(s_planned, 3)
            crooked = act.value_load(flag[0:1, 0:1], min_val=0, max_val=GROUPS)

            def stage(b):
                if not isinstance(b, int) or b > 0:
                    act.wait_ge(s_fin_turned, b)
                    act.wait_ge(s_total, b)
                act.activation(staged[:, :], aggr[:, bass.ds(b * P, P)], ACT.Copy).then_inc(s_staged, 1)
                act.activation(h_again[:, :], x_all[:, bass.ds(b, 1), :].rearrange("p o f -> p (o f)"), ACT.Relu,
                               bias=shift_all[:, bass.ds(b, 1)], scale=scale_all[:, bass.ds(b, 1)]
                               ).then_inc(s_h_again, 1)

            def deviate(b):
                act.wait_ge(s_o_var, b + 1)
                act.activation(o_dev[:, :], o_var[:, :], ACT.Sqrt).then_inc(s_o_dev, 1)

            with act.If(crooked < 1):
                def columns(i, u):
                    g, later = i * UNROLL + u, not isinstance(i, int) or i * UNROLL + u >= 2
                    act.wait_ge(s_edge_turned, g + 1)
                    if later:
                        act.wait_ge(s_pre, g - 1)
                    act.activation(edge_cols[:, u % 2, :], ps_edge[u % 2][:, :], ACT.Copy).then_inc(s_edge_cols, 1)
                    act.wait_ge(s_hot_turned, g + 1)
                    act.activation(onehot_cols[:, u % 2, :], ps_hot[u % 2][:, :], ACT.Copy).then_inc(s_hot_cols, 1)

                def relu(i, u):
                    act.wait_ge(s_z, i * UNROLL + u + 1)
                    act.activation(msg[:, u % 2, :, :], msg[:, u % 2, :, :], ACT.Relu).then_inc(s_msg, 1)

                def round_(i, last=False, finish=True):
                    for u in range(UNROLL):
                        if not (last and u == UNROLL - 1):
                            columns(i if u < UNROLL - 1 else i + 1, (u + 1) % UNROLL)
                        if finish and u == 3:
                            deviate(i - 2)
                        relu(i, u)
                        if finish and u == 1:
                            act.wait_ge(s_added, i * UNROLL)
                            stage(i - 2)

                columns(0, 0)
                round_(0, finish=False)
                round_(1, finish=False)
                with act.Fori(2, ROUNDS - 1) as i:
                    round_(i)
                round_(ROUNDS - 1, last=True)
                act.wait_ge(s_added, GROUPS)
                for b in (BLOCKS - 2, BLOCKS - 1):
                    stage(b)
                    deviate(b)
            with act.Else():
                with act.Fori(0, GROUPS) as g:
                    act.wait_ge(g_turned, g + 1)
                    act.activation(edge_cols[:, 0, :], ps_edge[0][:, :], ACT.Copy).then_inc(g_cols, 1)
                    act.wait_ge(g_z2, g + 1)
                    act.activation(msg[:, 0, :, :], msg[:, 0, :, :], ACT.Relu).then_inc(g_msg, 1)
                act.wait_ge(g_added, GROUPS * WIDES)
                with act.Fori(0, BLOCKS) as b:
                    act.wait_ge(s_fin_turned, b)
                    act.wait_ge(s_total, b)
                    stage(b)
                    deviate(b)

        @block.vector
        def _(dve):
            dve.wait_ge(s_ids, 16 * 2 * (2 + ROWS - (FULL_GROUPS - (QUADS - 1) * ROWS)))
            dve.tensor_copy(ids_f[0:ROWS, :, :, :], ids_i[0:ROWS, :, :, :]).then_inc(s_cast, 1)
            dve.wait_ge(s_cast, 1)
            dve.tensor_reduce(lowest[0:ROWS, :], ids_f[0:ROWS, 1, :, :], AX.X, ALU.min).then_inc(s_range, 1)
            dve.tensor_reduce(highest[0:ROWS, :], ids_f[0:ROWS, 1, :, :], AX.X, ALU.max).then_inc(s_range, 1)
            dve.wait_ge(s_range, 2)
            dve.wait_ge(s_const, 5)
            dve.tensor_tensor(highest[0:ROWS, :], highest[0:ROWS, :], lowest[0:ROWS, :], ALU.subtract
                              ).then_inc(s_range, 1)
            dve.tensor_tensor(floor_of[0:ROWS, :], lowest[0:ROWS, :], floor_of[0:ROWS, :], ALU.is_lt
                              ).then_inc(s_range, 1)
            for q in range(QUADS):
                ins = dve.tensor_scalar(diagonal[0:ROWS, q, 0:ROWS], ident[0:ROWS, 0:ROWS], lowest[0:ROWS, q:q + 1],
                                        None, ALU.mult)
            ins.then_inc(s_diag, 1)
            dve.wait_ge(s_range, 4)
            dve.tensor_scalar(highest[0:ROWS, :], highest[0:ROWS, :], float(WIN), None, ALU.is_ge
                              ).then_inc(s_range, 1)
            dve.wait_ge(s_range, 5)
            dve.tensor_tensor(bad[0:ROWS, :], highest[0:ROWS, :], floor_of[0:ROWS, :], ALU.max).then_inc(s_diag, 1)

            def keep_plan():
                dve.wait_ge(s_plan, 1)
                dve.tensor_copy(base_i[:, :], ps_sum[0:1, 0:GROUPS]).then_inc(s_planned, 1)
                dve.tensor_copy(flag[:, :], ps_fin[0:1, 0:1]).then_inc(s_planned, 1)
                dve.wait_ge(s_ids_kept, 2 * QUADS)
                dve.memset(dst_f[0:TAIL_DONE, FULL_GROUPS, :], -1.0)
                dve.memset(dst_f[:, FULL_GROUPS + 1:GROUPS, :], -1.0).then_inc(s_planned, 1)

            def statistics(c, par, half):
                extra = 16 if isinstance(half, int) and c == CHUNKS - 1 else 0
                dve.wait_ge(s_x[par], (half + 1) * 16 + extra)
                if not isinstance(c, int) or c > 0:
                    dve.wait_ge(s_norm, c)
                for k in range(CHUNK):
                    ins = dve.bn_stats(moments6[:, k, :],
                                       x_all[:, bass.ds(c * CHUNK + k, 1), :].rearrange("p o f -> p (o f)"))
                ins.then_inc(s_vec, 1)
                dve.wait_ge(s_vec, c * 3 + 1)
                dve.sem_inc(s_gate_dve, 1)
                for k in range(CHUNK):
                    ins = dve.bn_aggr(moments[:, k, :], moments6[:, k, :])
                ins.then_inc(s_vec, 1)
                dve.wait_ge(s_vec, c * 3 + 2)
                dve.tensor_scalar(moments[:, :, 1], moments[:, :, 1], EPS, None, ALU.add).then_inc(s_var, 1)

            def normalise(c):
                at = bass.ds(c * CHUNK, CHUNK)
                dve.wait_ge(s_dev, c + 1)
                dve.reciprocal(scale_all[:, at], deviation[:, :]).then_inc(s_vec, 1)
                dve.wait_ge(s_vec, c * 3 + 3)
                dve.scalar_tensor_tensor(out=shift_all[:, at], in0=moments[:, :, 0], scalar=-1.0,
                                         in1=scale_all[:, at], op0=ALU.mult, op1=ALU.mult).then_inc(s_norm, 1)

            def keep_b(c, par, half):
                dve.wait_ge(s_tab, c + 1)
                if not isinstance(half, int) or half > 0:
                    dve.wait_ge(s_b_stored[par], half * 16 + (0 if par else 16))
                for m in range(2):
                    nb = min(4, CHUNK - 4 * m)
                    ins = dve.tensor_tensor(b_out[:, par, 4 * m:4 * m + nb, :],
                                            ps_tab[2 + m][:, 0:nb * H].rearrange("p (b f) -> p b f", b=nb),
                                            b1_all[:, :].unsqueeze(1).to_broadcast([P, nb, H]), ALU.add)
                ins.then_inc(s_b_kept, 1)

            dve.wait_ge(s_weights, 96)
            statistics(0, 0, 0)
            normalise(0)
            statistics(1, 1, 0)
            keep_b(0, 0, 0)
            normalise(1)
            keep_plan()
            with dve.Fori(1, CHUNKS // 2 - 1) as half:
                statistics(half * 2, 0, half)
                keep_b(half * 2 - 1, 1, half - 1)
                normalise(half * 2)
                statistics(half * 2 + 1, 1, half)
                keep_b(half * 2, 0, half)
                normalise(half * 2 + 1)
            end = CHUNKS // 2 - 1
            statistics(CHUNKS - 2, 0, end)
            keep_b(CHUNKS - 3, 1, end - 1)
            normalise(CHUNKS - 2)
            statistics(CHUNKS - 1, 1, end)
            keep_b(CHUNKS - 2, 0, end)
            normalise(CHUNKS - 1)
            keep_b(CHUNKS - 1, 1, end)

            dve.wait_ge(s_planned, 3)
            crooked = dve.value_load(flag[0:1, 0:1], min_val=0, max_val=GROUPS)
            dve.wait_ge(s_zero, 1)
            dve.wait_ge(s_zero_row, 1)
            dve.wait_ge(s_b_stored[0], (CHUNKS // 2 + 1) * 16)

            def add_h(b):
                dve.wait_ge(s_fin_turned, b + 1)
                dve.wait_ge(s_h_again, b + 1)
                if not isinstance(b, int) or b > 0:
                    dve.wait_ge(s_o_vec, b * 6)
                dve.tensor_tensor(total[:, :], ps_fin[:, 0:P], h_again[:, :], ALU.add).then_inc(s_total, 1)
                dve.wait_ge(s_total, b + 1)
                dve.bn_stats(o_moments6[:, :], total[:, :]).then_inc(s_o_vec, 1)
                dve.wait_ge(s_o_vec, b * 6 + 1)
                dve.sem_inc(s_gate_dve, 1)
                dve.bn_aggr(o_moments[:, :], o_moments6[:, :]).then_inc(s_o_vec, 1)
                dve.wait_ge(s_o_vec, b * 6 + 2)
                if not isinstance(b, int) or b > 0:
                    dve.wait_ge(s_o_dev, b)
                dve.tensor_scalar(o_var[:, :], o_moments[:, 1:2], EPS, None, ALU.add).then_inc(s_o_var, 1)

            def finish(b):
                dve.wait_ge(s_o_dev, b + 1)
                dve.reciprocal(o_scale[:, :], o_dev[:, :]).then_inc(s_o_vec, 1)
                if not isinstance(b, int) or b > 0:
                    dve.wait_ge(s_out_stored, b * 16)
                dve.wait_ge(s_o_vec, b * 6 + 3)
                dve.tensor_scalar(out_rows[:, :], total[:, :], o_moments[:, 0:1], o_scale[:, 0:1],
                                  ALU.subtract, ALU.mult).then_inc(s_o_vec, 1)
                dve.wait_ge(s_o_vec, b * 6 + 4)
                dve.tensor_tensor(out_rows[:, :], out_rows[:, :], gamma_all[:, :], ALU.mult).then_inc(s_o_vec, 1)
                dve.wait_ge(s_o_vec, b * 6 + 5)
                dve.tensor_tensor(out_rows[:, :], out_rows[:, :], beta_all[:, :], ALU.add).then_inc(s_o_vec, 1)
                dve.wait_ge(s_o_vec, b * 6 + 6)
                dve.tensor_tensor(out_rows[:, :], out_rows[:, :],
                                  x_all[:, bass.ds(b, 1), :].rearrange("p o f -> p (o f)"), ALU.add).then_inc(s_out, 1)

            with dve.If(crooked < 1):
                dve.tensor_tensor(dst_f[:, :, :], dst_f[:, :, :],
                                  ps_sum[:, 0:GROUPS].unsqueeze(2).to_broadcast([P, GROUPS, SUB]),
                                  ALU.subtract).then_inc(s_rel, 1)
                dve.wait_ge(s_rel, 1)

                def pick(i, u):
                    dve.tensor_copy(picks[:, u, :], src_f[:, bass.ds(i * UNROLL + u, 1), :].rearrange("p o k -> p (o k)")
                                    ).then_inc(s_picks, 1)

                def one_hot(i, u):
                    if not isinstance(i, int) or i > 0:
                        dve.wait_ge(s_sum, (i - 1) * UNROLL + u + 1)
                    dve.tensor_tensor(
                        onehot[:, u, :, 0:WIN],
                        dst_f[:, bass.ds(i * UNROLL + u, 1), :].rearrange("p o k -> p (o k)").unsqueeze(2)
                        .to_broadcast([P, SUB, WIN]),
                        count[:, 0:WIN].unsqueeze(1).to_broadcast([P, SUB, WIN]),
                        ALU.is_equal).then_inc(s_hot, 1)

                def add_a(i, u):
                    g, later = i * UNROLL + u, not isinstance(i, int) or i * UNROLL + u >= 2
                    dve.wait_ge(s_pre, g + 1)
                    for k in range(SUB):
                        dve.wait_ge(s_a_rows[u][k], (i + 1) * 16)
                    if later:
                        dve.wait_ge(s_sum, g - 1)
                    dve.tensor_tensor(msg[:, u % 2, :, :].rearrange("p k f -> p (k f)"), ps_pre[u % 2][:, :],
                                      a_rows[:, u, :, :].rearrange("p k f -> p (k f)"), ALU.add).then_inc(s_z, 1)

                def add_sums(i, u):
                    g = i * UNROLL + u
                    dve.wait_ge(s_sum, g + 1)
                    if not isinstance(g, int) or g > 0:
                        dve.wait_ge(s_added, g)
                    base = dve.value_load(base_i[0:1, bass.ds(g, 1)], min_val=0, max_val=N - 1)
                    at = aggr[:, bass.ds(base, WIN)]
                    dve.tensor_tensor(at, ps_sums[u % 2], at, ALU.add
                                      ).then_inc(s_added, 1)

                def round_(i, first=False, last=False, finish_=True):
                    for u in range(UNROLL):
                        if not (last and u >= 2):
                            one_hot(i if u < 2 else i + 1, (u + 2) % UNROLL)
                        add_a(i, u)
                        if not last:
                            pick(i + 1, u)
                        if not (first and u == 0):
                            add_sums(i if u else i - 1, (u - 1) % UNROLL)
                        if finish_ and u == 2:
                            add_h(i - 2)
                        if finish_ and u == 3:
                            finish(i - 2)

                for u in range(UNROLL):
                    pick(0, u)
                one_hot(0, 0)
                one_hot(0, 1)
                round_(0, first=True, finish_=False)
                round_(1, finish_=False)
                with dve.Fori(2, ROUNDS - 1) as i:
                    round_(i)
                round_(ROUNDS - 1, last=True)
                add_sums(ROUNDS - 1, UNROLL - 1)
                for b in (BLOCKS - 2, BLOCKS - 1):
                    add_h(b)
                    finish(b)
            with dve.Else():
                with dve.Fori(0, GROUPS) as g:
                    senders = src_f[:, bass.ds(g, 1), :].rearrange("p o k -> p (o k)")
                    receivers = dst_f[:, bass.ds(g, 1), :].rearrange("p o k -> p (o k)")
                    for k in range(2 * SUB):
                        dve.wait_ge(g_rows[k], g * 16)
                    dve.tensor_copy(picks[:, 0, :], senders).then_inc(g_picks, 1)
                    dve.tensor_scalar(picks[:, 1, :], receivers, 0.0, None, ALU.max).then_inc(g_picks, 1)
                    dve.wait_ge(g_pre, g + 1)
                    for k in range(2 * SUB):
                        dve.wait_ge(g_rows[k], (g + 1) * 16)
                    dve.wait_ge(g_sum, g * WIDES)
                    z = msg[:, 0, :, :].rearrange("p k f -> p (k f)")
                    dve.tensor_tensor(z, ps_pre[0][:, :], a_rows[:, 0, :, :].rearrange("p k f -> p (k f)"),
                                      ALU.add).then_inc(g_z, 1)
                    dve.wait_ge(g_z, g + 1)
                    dve.tensor_tensor(z, z, a_rows[:, 1, :, :].rearrange("p k f -> p (k f)"), ALU.add
                                      ).then_inc(g_z2, 1)
                    with dve.Fori(0, WIDES) as w:
                        dve.wait_ge(g_added, g * WIDES + w)
                        for k in range(SUB):
                            ins = dve.tensor_scalar(onehot[:, k, :, :].rearrange("p k n -> p (k n)"), count[:, :],
                                                    receivers[:, k:k + 1], None, ALU.is_equal)
                        ins.then_inc(g_hot, 1)
                        dve.wait_ge(g_hot, g * WIDES + w + 1)
                        dve.tensor_scalar(receivers, receivers, -float(WIDE), None, ALU.add)
                        dve.wait_ge(g_sum, g * WIDES + w + 1)
                        at = aggr[:, bass.ds(w * WIDE, WIDE)]
                        dve.tensor_tensor(at, ps_sum[:, :], at, ALU.add).then_inc(g_added, 1)
                with dve.Fori(0, BLOCKS) as b:
                    dve.wait_ge(s_o_vec, b * 6)
                    dve.wait_ge(s_o_dev, b)
                    dve.wait_ge(s_out_stored, b * 16)
                    add_h(b)
                    finish(b)


_INS = ["x", "src", "dst", "edge_attr_128", "L0_gnn_W1", "L0_gnn_b1", "L0_gnn_ln_gamma", "L0_gnn_ln_beta"]


def kernel(**inputs):
    import numpy as _np
    import concourse.bacc as _bacc
    from concourse import mybir as _mybir
    from concourse.bass_utils import run_bass_kernel_spmd as _run

    nc = _bacc.Bacc("TRN2", target_bir_lowering=False, num_devices=1)
    arrays, args = {}, []
    for name in _INS:
        a = _np.ascontiguousarray(inputs[name])
        arrays[f"in_{name}"] = a
        args.append(nc.dram_tensor(f"in_{name}", a.shape, _mybir.dt.from_np(a.dtype), kind="ExternalInput").ap())
    shape = inputs["x"].shape
    args.append(nc.dram_tensor("out_0", shape, _mybir.dt.float32, kind="ExternalOutput").ap())
    build(nc, *args)
    r = _run(nc, [arrays], core_ids=[0])
    return r.results[0]["out_0"]
```

```python
from contextlib import ExitStack

import concourse.bass as bass
from concourse import mybir

F32 = mybir.dt.float32
I32 = mybir.dt.int32
ALU = mybir.AluOpType
ACT = mybir.ActivationFunctionType
AX = mybir.AxisListType

P = 128
H = 128
EPS = 1e-5
SUB = 4
GROUP = P * SUB
UNROLL = 4
WIN = 64
LEAD = 128
X_LEAD = 3
AHEAD = 5
WIDE = 512
CHUNK = 7


def past(value, n):
    return not isinstance(value, int) or value >= n


def build(nc, x, src, dst, edge_attr, w1, b1, gamma, beta, out):
    N, E = x.shape[0], edge_attr.shape[0]
    BLOCKS = -(-N // P)
    LAST_ROWS = N - (BLOCKS - 1) * P
    FULL_GROUPS = E // GROUP
    GROUPS = -(-E // GROUP)
    ROUNDS = -(-GROUPS // UNROLL)
    TAIL_START = E - GROUP
    TAIL_DONE = (FULL_GROUPS * GROUP - TAIL_START) // SUB
    QUADS = 4
    ROWS = -(-GROUPS // QUADS)
    ID_ROWS = QUADS * ROWS
    PER_GROUP = P // UNROLL
    CHUNKS = BLOCKS // CHUNK
    ALL_BLOCKS = ROUNDS - 1 + AHEAD
    WIDES = -(-(BLOCKS * P) // WIDE)
    ID_LOADS = 2 + ROWS - (FULL_GROUPS - (QUADS - 1) * ROWS)
    LEFT = GROUPS - (ROUNDS - 1) * UNROLL
    assert BLOCKS == ROUNDS and CHUNKS % 2 == 0 and CHUNKS * CHUNK == BLOCKS and CHUNKS >= 6
    assert E % SUB == 0 and FULL_GROUPS == GROUPS - 1 and ID_ROWS == GROUPS + 1 and ROWS <= P
    assert LEFT == 3 and WIDES * WIDE <= ALL_BLOCKS * P and AHEAD <= CHUNK
    assert PER_GROUP * (UNROLL - 1) + LEAD + WIN <= 3 * P

    table_a = nc.dram_tensor("table_a", (BLOCKS * P, H), F32)
    table_b = nc.dram_tensor("table_b", (ALL_BLOCKS * P, H), F32)

    ctx = ExitStack()
    with ctx:
        def sb(name, shape, dt=F32):
            return ctx.enter_context(nc.sbuf_tensor(name, shape, dt))

        def bank(name):
            return ctx.enter_context(nc.psum_tensor(name, [P, 512], F32))

        def sem(name):
            return ctx.enter_context(nc.semaphore(name))

        x_all = sb("x_all", [P, ALL_BLOCKS, H])
        aggr = sb("aggr", [P, ALL_BLOCKS * P])
        src_f = sb("src_f", [P, ID_ROWS, SUB])
        dst_f = sb("dst_f", [P, ID_ROWS, SUB])
        base_all = sb("base_all", [P, ID_ROWS])
        base_i = sb("base_i", [1, ID_ROWS], I32)
        scale_all = sb("scale_all", [P, ALL_BLOCKS])
        shift_all = sb("shift_all", [P, ALL_BLOCKS])
        ident = sb("ident", [P, P])
        ones = sb("ones", [P, P])
        zeros = sb("zeros", [P, P])
        eps = sb("eps", [P, 1])
        count = sb("count", [P, WIDE])
        w_a = sb("w_a", [P, H])
        w_b = sb("w_b", [P, H])
        w_c = sb("w_c", [P, H])
        b1_all = sb("b1_all", [P, H])
        gamma_all = sb("gamma_all", [P, H])
        beta_all = sb("beta_all", [P, H])
        flag = sb("flag", [1, 1], I32)
        centred = sb("centred", [P, 2, CHUNK, H])
        mean_all = sb("mean_all", [P, BLOCKS])
        h_cols = sb("h_cols", [P, 2, CHUNK, P])
        a_out = sb("a_out", [P, 2, CHUNK, H])
        b_first = sb("b_first", [P, AHEAD, H])
        halves = sb("halves", [P, 2, CHUNK, 6])
        pair_sum = sb("pair_sum", [P, 2, CHUNK, 2])
        pair_gap = sb("pair_gap", [P, CHUNK])
        gap_sq = sb("gap_sq", [P, CHUNK])
        sum_sq = sb("sum_sq", [P, CHUNK])
        four_var = sb("four_var", [P, CHUNK])
        deviation = sb("deviation", [P, CHUNK])
        ids_at = ALL_BLOCKS * P - 4 * QUADS * GROUP
        ids_i = aggr[:, ids_at:ids_at + 2 * QUADS * GROUP].bitcast(I32).rearrange(
            "p (a q e) -> p a q e", a=2, q=QUADS)
        ids_f = aggr[:, ids_at + 2 * QUADS * GROUP:].rearrange("p (a q e) -> p a q e", a=2, q=QUADS)
        lowest = sb("lowest", [P, QUADS])
        highest = sb("highest", [P, QUADS])
        even = sb("even", [P, QUADS])
        bad = sb("bad", [P, QUADS])
        diagonal = sb("diagonal", [P, QUADS, P])
        edges = sb("edges", [P, UNROLL, GROUP])
        a_rows = sb("a_rows", [P, UNROLL, SUB, H])
        b_win = sb("b_win", [P, UNROLL, H])
        picks = sb("picks", [P, UNROLL, SUB], I32)
        onehot = sb("onehot", [P, 4, SUB, P])
        edge_cols = sb("edge_cols", [P, 2, GROUP])
        onehot_cols = sb("onehot_cols", [P, 2, GROUP])
        msg = sb("msg", [P, 2, SUB, H])
        hb_rows = sb("hb_rows", [P, H])
        hb_cols = sb("hb_cols", [P, P])
        b_rows = sb("b_rows", [P, H])
        staged = sb("staged", [P, P])
        h_again = sb("h_again", [P, H])
        total = sb("total", [P, H])
        out_rows = sb("out_rows", [P, H])
        o_halves = sb("o_halves", [P, 6])
        o_moments = sb("o_moments", [P, 2])
        o_dev = sb("o_dev", [P, 1])
        o_scale = sb("o_scale", [P, 1])

        ps_edge = [bank("ps_edge0"), bank("ps_edge1")]
        ps_hot = [bank("ps_hot0"), bank("ps_hot1")]
        ps_pre = [bank("ps_pre0"), bank("ps_pre1")]
        ps_sum = bank("ps_sum")
        ps_fin = bank("ps_fin")
        ps_sums = [ps_sum[:, 0:WIN], ps_fin[:, P:P + WIN]]
        ps_total, ps_hb, ps_b = ps_fin[:, 0:P], ps_fin[:, 2 * P:3 * P], ps_fin[:, 3 * P:4 * P]
        ps_turn = [[ps_edge[0], ps_edge[1]], [ps_hot[0], ps_hot[1]]]
        ps_tab = [[ps_pre[0], ps_pre[1]], [ps_sum, ps_fin]]
        ps_first = ps_hot
        ps_base, ps_bad = ps_edge[0], ps_edge[1][0:1, 0:1]
        ps_ids = [[ps_pre[0], ps_pre[1], ps_sum, ps_fin], [ps_hot[0], ps_hot[1], ps_edge[0], ps_edge[1]]]

        s_w_a = sem("s_w_a")
        s_weights = sem("s_weights")
        s_ids = [sem("s_ids_src"), sem("s_ids_dst")]
        s_x = [sem("s_x0"), sem("s_x1")]
        s_pad = sem("s_pad")
        s_const = sem("s_const")
        s_cast = [sem("s_cast_src"), sem("s_cast_dst")]
        s_range = sem("s_range")
        s_diag = sem("s_diag")
        s_bad = sem("s_bad")
        s_ids_turned = sem("s_ids_turned")
        s_ids_kept = sem("s_ids_kept")
        s_plan = sem("s_plan")
        s_planned = sem("s_planned")
        s_vec = sem("s_vec")
        s_gap = sem("s_gap")
        s_var = sem("s_var")
        s_dev = sem("s_dev")
        s_mean = sem("s_mean")
        s_scale = sem("s_scale")
        s_norm = sem("s_norm")
        s_centred = sem("s_centred")
        s_centred_last = sem("s_centred_last")
        s_turned = sem("s_turned")
        s_h_cols = sem("s_h_cols")
        s_tab = sem("s_tab")
        s_a_kept = [sem("s_a_kept_dve"), sem("s_a_kept_act")]
        s_a_stored = [sem("s_a_stored0"), sem("s_a_stored1")]
        s_b_first = sem("s_b_first")
        s_b_first_kept = sem("s_b_first_kept")
        s_b_stored = sem("s_b_stored")
        s_zero = sem("s_zero")
        s_gate_pool = sem("s_gate_pool")
        s_gate_dve = sem("s_gate_dve")
        s_edges = [sem(f"s_edges{u}") for u in range(UNROLL)]
        s_b_win = [sem(f"s_b_win{u}") for u in range(UNROLL)]
        s_a_rows = [[sem(f"s_a_rows{u}_{k}") for k in range(SUB)] for u in range(UNROLL)]
        s_picks = sem("s_picks")
        s_rel = sem("s_rel")
        s_hot = sem("s_hot")
        s_edge_turned = sem("s_edge_turned")
        s_hot_turned = sem("s_hot_turned")
        s_edge_cols = sem("s_edge_cols")
        s_hot_cols = sem("s_hot_cols")
        s_pre = sem("s_pre")
        s_z = sem("s_z")
        s_msg = sem("s_msg")
        s_sum = sem("s_sum")
        s_added = sem("s_added")
        s_hb = sem("s_hb")
        s_hb_turned = sem("s_hb_turned")
        s_hb_cols = sem("s_hb_cols")
        s_b_tab = sem("s_b_tab")
        s_b_kept = sem("s_b_kept")
        s_staged = sem("s_staged")
        s_h_again = sem("s_h_again")
        s_fin_turned = sem("s_fin_turned")
        s_total = sem("s_total")
        s_o_vec = sem("s_o_vec")
        s_o_var = sem("s_o_var")
        s_o_dev = sem("s_o_dev")
        s_out = sem("s_out")
        s_out_stored = sem("s_out_stored")
        g_edges = sem("g_edges")
        g_picks = sem("g_picks")
        g_rows = [sem(f"g_rows{k}") for k in range(2 * SUB)]
        g_turned = sem("g_turned")
        g_cols = sem("g_cols")
        g_pre = sem("g_pre")
        g_z = sem("g_z")
        g_z2 = sem("g_z2")
        g_msg = sem("g_msg")
        g_hot = sem("g_hot")
        g_rel = sem("g_rel")
        g_sum = sem("g_sum")
        g_added = sem("g_added")

        block = ctx.enter_context(nc.Block())

        def first_block(c):
            return 0 if isinstance(c, int) and c == CHUNKS - 1 else c * CHUNK + CHUNK

        def node_rows(tensor, c):
            return tensor[bass.ds(first_block(c) * P, CHUNK * P), :].rearrange("(b p) f -> p b f", p=P)

        def group_rows(start):
            return edge_attr[bass.ds(start, GROUP), :].rearrange("(p k) f -> p (k f)", p=P)

        def start_of(i, u):
            if isinstance(i, int) and i * UNROLL + u >= FULL_GROUPS:
                return TAIL_START
            return i * (UNROLL * GROUP) + u * GROUP

        def x_block(b):
            return x_all[:, bass.ds(b, 1), :].rearrange("p o f -> p (o f)")

        def before(i, u):
            return (i, u - 1) if u else (i - 1, UNROLL - 1)

        def after(i, u, n):
            return (i, u + n) if u + n < UNROLL else (i + 1, u + n - UNROLL)


        @block.sync
        def _(sp):
            def load_x(c, par):
                if not isinstance(c, int) or c != CHUNKS - 2:
                    sp.dma_start(x_all[:, bass.ds(first_block(c), CHUNK), :], node_rows(x, c)).then_inc(s_x[par], 16)
                else:
                    first = first_block(c)
                    sp.dma_start(x_all[:, first:BLOCKS - 1, :],
                                 x[first * P:(BLOCKS - 1) * P, :].rearrange("(b p) f -> p b f", p=P)
                                 ).then_inc(s_x[par], 16)
                    sp.wait_ge(s_pad, 1)
                    sp.dma_start(x_all[0:LAST_ROWS, BLOCKS - 1, :], x[(BLOCKS - 1) * P:N, :]
                                 ).then_inc(s_x[par], 16)

            def load_ids(a, ids):
                full = FULL_GROUPS - (QUADS - 1) * ROWS
                sp.dma_start(ids_i[0:ROWS, a, 0:QUADS - 1, :],
                             ids[0:(QUADS - 1) * ROWS * GROUP].rearrange("(q r e) -> r q e", q=QUADS - 1, r=ROWS)
                             ).then_inc(s_ids[a], 16)
                sp.dma_start(ids_i[0:full, a, QUADS - 1, :],
                             ids[(QUADS - 1) * ROWS * GROUP:FULL_GROUPS * GROUP].rearrange("(r e) -> r e", r=full)
                             ).then_inc(s_ids[a], 16)
                for r in range(full, ROWS):
                    sp.dma_start(ids_i[r:r + 1, a, QUADS - 1, :],
                                 ids[TAIL_START:E].rearrange("(r e) -> r e", r=1)).then_inc(s_ids[a], 16)

            def next_x(pair, par):
                sp.wait_ge(s_x[par], pair * 16)
                load_x(pair * 2 + par, par)

            def store_a(pair, par):
                for kept in s_a_kept:
                    sp.wait_ge(kept, pair * 2 + par + 1)
                sp.dma_start(node_rows(table_a, pair * 2 + par), a_out[:, par, :, :]).then_inc(s_a_stored[par], 16)

            load_x(0, 0)
            load_x(1, 1)
            sp.dma_start(w_a[:, :], w1[0:H, :]).then_inc(s_w_a, 16)
            load_ids(1, dst)
            next_x(1, 0)
            next_x(1, 1)
            sp.dma_start(w_b[:, :], w1[H:2 * H, :]).then_inc(s_weights, 16)
            sp.dma_start(w_c[:, :], w1[2 * H:3 * H, :]).then_inc(s_weights, 16)
            for tile, row in ((b1_all, b1), (gamma_all, gamma), (beta_all, beta)):
                sp.dma_start(tile[:, :], row.rearrange("(o f) -> o f", o=1).to_broadcast([P, H])
                             ).then_inc(s_weights, 16)
            for pair in range(2, X_LEAD):
                for par in range(2):
                    next_x(pair, par)
            load_ids(0, src)
            with sp.Fori(0, CHUNKS // 2 - 1 - X_LEAD) as pair:
                for par in range(2):
                    store_a(pair, par)
                    next_x(pair + X_LEAD, par)
            for par in range(2):
                store_a(CHUNKS // 2 - 1 - X_LEAD, par)
                next_x(CHUNKS // 2 - 1, par)
            with sp.Fori(CHUNKS // 2 - X_LEAD, CHUNKS // 2 - 1) as pair:
                for par in range(2):
                    store_a(pair, par)
            for par in range(2):
                store_a(CHUNKS // 2 - 1, par)

            sp.wait_ge(s_planned, 2)
            crooked = sp.value_load(flag[0:1, 0:1], min_val=0, max_val=ID_ROWS)

            with sp.If(crooked < 1):
                def step(i, u):
                    g = i * UNROLL + u
                    if past(i, 1):
                        sp.wait_ge(s_edge_turned, g - UNROLL + 1)
                    sp.dma_start(edges[:, u, :], group_rows(start_of(i, u))).then_inc(s_edges[u], 16)
                    if past(i, 1):
                        sp.wait_ge(s_pre, g - UNROLL + 1)
                    if u == 0:
                        sp.wait_ge(s_b_stored, 16 if isinstance(i, int) and i < 2 else (i - 1) * 16)
                    base = sp.value_load(base_i[0:1, bass.ds(g, 1)], min_val=0, max_val=N - 1)
                    sp.dma_start(b_win[0:WIN, u, :], table_b[bass.ds(base, WIN), :]).then_inc(s_b_win[u], 16)

                sp.wait_ge(s_zero, 1)
                for i in range(3):
                    for u in range(UNROLL):
                        step(i, u)
                with sp.Fori(3, ROUNDS - 1) as i:
                    for u in range(UNROLL):
                        step(i, u)
                    sp.wait_ge(s_out, i - 2)
                    sp.dma_start(out[bass.ds((i - 3) * P, P), :], out_rows[:, :]).then_inc(s_out_stored, 16)
                for u in range(LEFT):
                    step(ROUNDS - 1, u)
                for b in range(ROUNDS - 4, BLOCKS):
                    rows = P if b < BLOCKS - 1 else LAST_ROWS
                    sp.wait_ge(s_out, b + 1)
                    sp.dma_start(out[b * P:b * P + rows, :], out_rows[0:rows, :]).then_inc(s_out_stored, 16)
                sp.wait_ge(s_b_stored, (ROUNDS - 1) * 16)
                sp.wait_ge(s_out_stored, BLOCKS * 16)
            with sp.Else():
                def load(g, start):
                    if past(g, 1):
                        sp.wait_ge(g_turned, g)
                    sp.dma_start(edges[:, 0, :], group_rows(start)).then_inc(g_edges, 16)

                load(0, 0)
                with sp.Fori(1, FULL_GROUPS) as g:
                    load(g, g * GROUP)
                load(FULL_GROUPS, TAIL_START)
                with sp.Fori(0, BLOCKS - 1) as b:
                    sp.wait_ge(s_out, b + 1)
                    sp.dma_start(out[bass.ds(b * P, P), :], out_rows[:, :]).then_inc(s_out_stored, 16)
                sp.wait_ge(s_out, BLOCKS)
                sp.dma_start(out[(BLOCKS - 1) * P:N, :], out_rows[0:LAST_ROWS, :]).then_inc(s_out_stored, 16)
                sp.wait_ge(s_out_stored, BLOCKS * 16)

        @block.gpsimd
        def _(pool):
            pool.memset(ident[:, :], 0.0).then_inc(s_const, 1)
            pool.memset(ones[:, :], 1.0).then_inc(s_const, 1)
            pool.iota(even[:, :], pattern=[[ROWS * PER_GROUP, QUADS]], base=0, channel_multiplier=PER_GROUP,
                      allow_small_or_imprecise_dtypes=True).then_inc(s_const, 1)
            pool.memset(eps[:, :], EPS).then_inc(s_const, 1)
            pool.wait_ge(s_const, 4)
            pool.affine_select(out=ident[:, :], in_=ident[:, :], compare_op=ALU.not_equal, fill=1.0,
                               base=0, pattern=[[-1, P]], channel_multiplier=1).then_inc(s_const, 1)
            pool.memset(x_all[:, BLOCKS - 1:ALL_BLOCKS, :], 0.0).then_inc(s_pad, 1)
            pool.iota(count[:, :], pattern=[[1, WIDE]], base=0, channel_multiplier=0,
                      allow_small_or_imprecise_dtypes=True)
            pool.memset(scale_all[:, BLOCKS:ALL_BLOCKS], 0.0)
            pool.memset(shift_all[:, BLOCKS:ALL_BLOCKS], 0.0)
            pool.memset(zeros[:, :], 0.0)
            pool.memset(b_win[:, :, :], 0.0)
            pool.memset(onehot[:, :, :, :], 0.0).then_inc(s_zero, 1)

            def chunk(c, par):
                pool.wait_ge(s_mean, c + 1)
                if past(c, 2):
                    pool.wait_ge(s_turned, c - 1)
                n = 4 if isinstance(c, int) and c == CHUNKS - 1 else CHUNK
                pool.tensor_tensor(centred[:, par, 0:n, :], x_all[:, bass.ds(first_block(c), n), :],
                                   mean_all[:, bass.ds(first_block(c), n)].unsqueeze(2).to_broadcast([P, n, H]),
                                   ALU.subtract).then_inc(s_centred, 1)
                pool.tensor_tensor(pair_gap[:, :], halves[:, par, :, 1], halves[:, par, :, 4], ALU.subtract
                                   ).then_inc(s_gap, 1)
                pool.wait_ge(s_gap, c * 3 + 1)
                pool.tensor_tensor(gap_sq[:, :], pair_gap[:, :], pair_gap[:, :], ALU.mult).then_inc(s_gap, 1)
                pool.tensor_scalar(sum_sq[:, :], pair_sum[:, par, :, 1], 4.0 / H, None, ALU.mult).then_inc(s_gap, 1)
                pool.wait_ge(s_gap, c * 3 + 3)
                if past(c, 1):
                    pool.wait_ge(s_dev, c)
                pool.tensor_tensor(four_var[:, :], sum_sq[:, :], gap_sq[:, :], ALU.add).then_inc(s_var, 1)

            chunk(0, 0)
            chunk(1, 1)
            with pool.Fori(1, CHUNKS // 2 - 1) as pair:
                for par in range(2):
                    chunk(pair * 2 + par, par)
            chunk(CHUNKS - 2, 0)
            chunk(CHUNKS - 1, 1)

            pool.wait_ge(s_ids[0], ID_LOADS * 16)
            for q in range(2):
                pool.tensor_copy(ids_f[0:ROWS, 0, q, :], ids_i[0:ROWS, 0, q, :]).then_inc(s_cast[0], 1)
            pool.wait_ge(s_range, 1)
            pool.tensor_tensor(diagonal[0:ROWS, :, 0:ROWS],
                               ident[0:ROWS, 0:ROWS].unsqueeze(1).to_broadcast([ROWS, QUADS, ROWS]),
                               lowest[0:ROWS, :].unsqueeze(2).to_broadcast([ROWS, QUADS, ROWS]), ALU.mult
                               ).then_inc(s_diag, 1)
            pool.wait_ge(s_b_first_kept, 1)
            pool.wait_ge(s_weights, 80)
            pool.tensor_tensor(b_first[:, :, :], b_first[:, :, :],
                               b1_all[:, :].unsqueeze(1).to_broadcast([P, AHEAD, H]), ALU.add
                               ).then_inc(s_b_first_kept, 1)

            pool.wait_ge(s_planned, 1)
            crooked = pool.value_load(flag[0:1, 0:1], min_val=0, max_val=ID_ROWS)
            for par in range(2):
                pool.wait_ge(s_a_stored[par], (CHUNKS // 2) * 16)

            with pool.If(crooked < 1):
                def step(i, u):
                    pool.wait_ge(s_picks, i * UNROLL + u + 1)
                    if past(i, 1):
                        pool.wait_ge(s_z, (i - 1) * UNROLL + u + 1)
                    pool.sem_inc(s_gate_pool, 1)
                    for k in range(SUB):
                        pool.indirect_dma_start(
                            a_rows[:, u, k, :], None, table_a[:, :],
                            bass.IndirectOffsetOnAxis(ap=picks[:, u, k:k + 1], axis=0),
                        ).then_inc(s_a_rows[u][k], 16)

                for u in range(UNROLL):
                    step(0, u)
                with pool.Fori(1, ROUNDS - 1) as i:
                    for u in range(UNROLL):
                        step(i, u)
                for u in range(LEFT):
                    step(ROUNDS - 1, u)
            with pool.Else():
                pool.wait_ge(s_b_stored, ROUNDS * 16)
                with pool.Fori(0, GROUPS) as g:
                    pool.wait_ge(g_picks, (g + 1) * 2)
                    pool.sem_inc(s_gate_pool, 1)
                    for k in range(SUB):
                        pool.indirect_dma_start(
                            a_rows[:, 0, k, :], None, table_a[:, :],
                            bass.IndirectOffsetOnAxis(ap=picks[:, 0, k:k + 1], axis=0),
                        ).then_inc(g_rows[k], 16)
                        pool.indirect_dma_start(
                            a_rows[:, 1, k, :], None, table_b[:, :],
                            bass.IndirectOffsetOnAxis(ap=picks[:, 1, k:k + 1], axis=0),
                        ).then_inc(g_rows[SUB + k], 16)
                    pool.wait_ge(g_z2, g + 1)

        @block.tensor
        def _(pe):
            pe.wait_ge(s_const, 5)

            def turn_ids(a, q):
                for k in range(SUB):
                    mm = pe.transpose(ps_ids[a][q][:, k * ROWS:(k + 1) * ROWS],
                                      ids_f[0:ROWS, a, q, k::SUB], ident[0:ROWS, 0:ROWS])
                mm.then_inc(s_ids_turned, 1)

            def turn_chunk(c, par):
                pe.wait_ge(s_centred, c + 1)
                if past(c, 2):
                    pe.wait_ge(s_h_cols, c - 1)
                for k in range(CHUNK):
                    if k == 4 and isinstance(c, int) and c == CHUNKS - 1:
                        pe.wait_ge(s_centred_last, 1)
                    mm = pe.transpose(ps_turn[par][k // 4][:, (k % 4) * P:(k % 4 + 1) * P],
                                      centred[:, par, k, :], ident[:, :])
                mm.then_inc(s_turned, 1)

            def table_chunk(c, par):
                pe.wait_ge(s_h_cols, c + 1)
                if past(c, 2):
                    for kept in s_a_kept:
                        pe.wait_ge(kept, c - 1)
                for k in range(CHUNK):
                    mm = pe.matmul(ps_tab[par][k // 4][:, (k % 4) * H:(k % 4 + 1) * H],
                                   h_cols[:, par, k, :], w_a[:, :], start=True, stop=True)
                mm.then_inc(s_tab, 1)

            turn_chunk(0, 0)
            pe.wait_ge(s_w_a, 16)
            for c in range(1, 4):
                turn_chunk(c, c % 2)
                table_chunk(c - 1, (c - 1) % 2)
            pe.wait_ge(s_weights, 80)
            with pe.Fori(2, CHUNKS // 2 - 1) as pair:
                for par in range(2):
                    turn_chunk(pair * 2 + par, par)
                    table_chunk(pair * 2 + par - 1, 1 - par)
            for c in range(CHUNKS - 2, CHUNKS):
                turn_chunk(c, c % 2)
                table_chunk(c - 1, (c - 1) % 2)
            table_chunk(CHUNKS - 1, 1)
            pe.wait_ge(s_cast[0], 1)
            for kept in s_a_kept:
                pe.wait_ge(kept, CHUNKS - 1)
            turn_ids(0, 0)
            for k in range(AHEAD):
                mm = pe.matmul(ps_first[k // 4][:, (k % 4) * H:(k % 4 + 1) * H],
                               h_cols[:, 1, k, :], w_b[:, :], start=True, stop=True)
            mm.then_inc(s_b_first, 1)
            pe.wait_ge(s_diag, 1)
            for q in range(QUADS):
                pe.matmul(ps_base[:, q * ROWS:(q + 1) * ROWS], ones[0:ROWS, :], diagonal[0:ROWS, q, 0:ROWS],
                          start=True, stop=True)
            pe.wait_ge(s_bad, 1)
            for q in range(QUADS):
                mm = pe.matmul(ps_bad, bad[0:ROWS, q:q + 1], ones[0:ROWS, 0:1],
                               start=(q == 0), stop=(q == QUADS - 1))
            mm.then_inc(s_plan, 1)
            pe.wait_ge(s_cast[0], 3)
            turn_ids(0, 1)
            for kept in s_a_kept:
                pe.wait_ge(kept, CHUNKS)
            turn_ids(0, 2)
            turn_ids(0, 3)
            pe.wait_ge(s_b_first_kept, 1)
            pe.wait_ge(s_cast[1], 1)
            turn_ids(1, 0)
            turn_ids(1, 1)
            pe.wait_ge(s_planned, 3)
            turn_ids(1, 2)
            turn_ids(1, 3)

            pe.wait_ge(s_planned, 1)
            crooked = pe.value_load(flag[0:1, 0:1], min_val=0, max_val=ID_ROWS)
            pe.wait_ge(s_ids_kept, 2 * QUADS)

            def turn_total(b):
                pe.wait_ge(s_staged, b + 1)
                if past(b, 1):
                    pe.wait_ge(s_total, b)
                pe.transpose(ps_total, staged[:, :], ident[:, :]).then_inc(s_fin_turned, 1)

            def turn_hb(j):
                pe.wait_ge(s_hb, j + 1)
                if past(j, 1):
                    pe.wait_ge(s_b_kept, j)
                pe.transpose(ps_hb, hb_rows[:, :], ident[:, :]).then_inc(s_hb_turned, 1)

            def table_b_block(j):
                pe.wait_ge(s_hb_cols, j + 1)
                pe.matmul(ps_b, hb_cols[:, :], w_b[:, :], start=True, stop=True).then_inc(s_b_tab, 1)

            with pe.If(crooked < 1):
                def turn(i, u):
                    g = i * UNROLL + u
                    pe.wait_ge(s_edges[u], (i + 1) * 16)
                    if past(g, 2):
                        pe.wait_ge(s_edge_cols, g - 1)
                    for k in range(SUB):
                        mm = pe.transpose(ps_edge[u % 2][:, k * P:(k + 1) * P],
                                          edges[:, u, k * H:(k + 1) * H], ident[:, :])
                    mm.then_inc(s_edge_turned, 1)
                    pe.wait_ge(s_hot, g + 1)
                    if past(g, 2):
                        pe.wait_ge(s_hot_cols, g - 1)
                    for k in range(SUB):
                        mm = pe.transpose(ps_hot[u % 2][:, k * P:(k + 1) * P], onehot[:, u, k, :], ident[:, :])
                    mm.then_inc(s_hot_turned, 1)

                def products(i, u):
                    g = i * UNROLL + u
                    pe.wait_ge(s_edge_cols, g + 1)
                    pe.wait_ge(s_hot_cols, g + 1)
                    pe.wait_ge(s_b_win[u], (i + 1) * 16)
                    if past(g, 2):
                        pe.wait_ge(s_z, g - 1)
                    for k in range(SUB):
                        to = ps_pre[u % 2][:, k * H:(k + 1) * H]
                        pe.matmul(to, edge_cols[:, u % 2, k * P:(k + 1) * P], w_c[:, :], start=True, stop=False)
                        mm = pe.matmul(to, onehot_cols[:, u % 2, k * P:(k + 1) * P], b_win[:, u, :],
                                       start=False, stop=True)
                    mm.then_inc(s_pre, 1)

                def sums(i, u):
                    g = i * UNROLL + u
                    pe.wait_ge(s_msg, g + 1)
                    if past(g, 2):
                        pe.wait_ge(s_added, g - 1)
                    for k in range(SUB):
                        mm = pe.matmul(ps_sums[u % 2], msg[:, u % 2, k, :], onehot[:, u, k, 0:WIN],
                                       start=(k == 0), stop=(k == SUB - 1))
                    mm.then_inc(s_sum, 1)

                def round_(i, groups=UNROLL):
                    last = groups < UNROLL
                    for u in range(groups):
                        if not (last and u == groups - 1):
                            turn(*after(i, u, 1))
                        products(i, u)
                        if u == 0 and past(i, 1):
                            if past(i, 3):
                                pe.wait_ge(s_total, i - 2)
                            table_b_block(i - 1)
                        if u == 2:
                            if past(i, 1):
                                pe.wait_ge(s_added, i * UNROLL)
                            if past(i, 2):
                                turn_total(i - 2)
                            if not last:
                                turn_hb(i)
                        if past(i * UNROLL + u, 1):
                            sums(*before(i, u))

                turn(0, 0)
                round_(0)
                round_(1)
                round_(2)
                with pe.Fori(3, ROUNDS - 1) as i:
                    round_(i)
                round_(ROUNDS - 1, LEFT)
                sums(ROUNDS - 1, LEFT - 1)
                for b in (BLOCKS - 2, BLOCKS - 1):
                    turn_total(b)
            with pe.Else():
                turn_hb(0)
                table_b_block(0)
                with pe.Fori(1, ROUNDS - 1) as j:
                    turn_hb(j)
                    table_b_block(j)
                with pe.Fori(0, GROUPS) as g:
                    pe.wait_ge(g_edges, (g + 1) * 16)
                    for k in range(SUB):
                        mm = pe.transpose(ps_edge[0][:, k * P:(k + 1) * P],
                                          edges[:, 0, k * H:(k + 1) * H], ident[:, :])
                    mm.then_inc(g_turned, 1)
                    pe.wait_ge(g_cols, g + 1)
                    for k in range(SUB):
                        mm = pe.matmul(ps_pre[0][:, k * H:(k + 1) * H], edge_cols[:, 0, k * P:(k + 1) * P],
                                       w_c[:, :], start=True, stop=True)
                    mm.then_inc(g_pre, 1)
                    with pe.Fori(0, WIDES) as w:
                        pe.wait_ge(g_msg, g + 1)
                        pe.wait_ge(g_added, g * WIDES + w + 1)
                        pe.wait_ge(g_hot, g * WIDES + w + 1)
                        for k in range(SUB):
                            mm = pe.matmul(ps_sum[:, :], msg[:, 0, k, :], onehot[:, k, :, :],
                                           start=(k == 0), stop=(k == SUB - 1))
                        mm.then_inc(g_sum, 1)
                turn_total(0)
                with pe.Fori(1, BLOCKS) as b:
                    turn_total(b)

        @block.scalar
        def _(act):
            act.wait_ge(s_const, 5)

            def deviate_chunk(c):
                act.wait_ge(s_var, c + 1)
                if past(c, 1):
                    act.wait_ge(s_scale, c)
                act.activation(deviation[:, :], four_var[:, :], ACT.Sqrt, bias=eps[:, 0:1], scale=0.25
                               ).then_inc(s_dev, 1)

            def h_columns(c, par):
                act.wait_ge(s_turned, c + 1)
                if past(c, 2):
                    act.wait_ge(s_tab, c - 1)
                act.activation(h_cols[:, par, 0:4, :].rearrange("p b n -> p (b n)"), ps_turn[par][0][:, :], ACT.Relu)
                act.activation(h_cols[:, par, 4:CHUNK, :].rearrange("p b n -> p (b n)"),
                               ps_turn[par][1][:, 0:(CHUNK - 4) * P], ACT.Relu).then_inc(s_h_cols, 1)

            def keep_a(c, par, half):
                act.wait_ge(s_tab, c + 1)
                if past(half, 1):
                    act.wait_ge(s_a_stored[par], half * 16)
                act.wait_ge(s_scale, c + 1)
                for k in range(4, CHUNK):
                    ins = act.activation(a_out[:, par, k, :], ps_tab[par][1][:, (k - 4) * H:(k - 3) * H],
                                         ACT.Copy, scale=scale_all[:, bass.ds(first_block(c) + k, 1)])
                ins.then_inc(s_a_kept[1], 1)

            def cast_ids(a, first):
                act.wait_ge(s_ids[a], ID_LOADS * 16)
                act.activation(ids_f[0:ROWS, a, first:, :], ids_i[0:ROWS, a, first:, :], ACT.Copy
                               ).then_inc(s_cast[a], 1)

            def keep_ids(a, ids, at, quads):
                for q in quads:
                    act.wait_ge(s_ids_turned, at + q + 1)
                    act.activation(ids[:, q * ROWS:(q + 1) * ROWS, :].rearrange("p r k -> p k r"),
                                   ps_ids[a][q][:, 0:SUB * ROWS].rearrange("p (k r) -> p k r", k=SUB),
                                   ACT.Copy).then_inc(s_ids_kept, 1)

            act.activation(o_dev[:, :], eps[:, :], ACT.Sqrt)
            cast_ids(1, 0)
            h_columns(0, 0)
            deviate_chunk(0)
            for c in range(1, 4):
                h_columns(c, c % 2)
                deviate_chunk(c)
                keep_a(c - 1, (c - 1) % 2, (c - 1) // 2)
            with act.Fori(2, CHUNKS // 2 - 1) as pair:
                for par in range(2):
                    c = pair * 2 + par
                    h_columns(c, par)
                    deviate_chunk(c)
                    keep_a(c - 1, 1 - par, pair - 1 + par)
            for c in range(CHUNKS - 2, CHUNKS):
                h_columns(c, c % 2)
                deviate_chunk(c)
                keep_a(c - 1, (c - 1) % 2, (c - 1) // 2)
            keep_a(CHUNKS - 1, 1, CHUNKS // 2 - 1)
            keep_ids(0, src_f, 0, range(1))
            act.wait_ge(s_b_first, 1)
            for k in range(AHEAD):
                ins = act.activation(b_first[:, k, :], ps_first[k // 4][:, (k % 4) * H:(k % 4 + 1) * H],
                                     ACT.Copy, scale=scale_all[:, k:k + 1])
            ins.then_inc(s_b_first_kept, 1)
            cast_ids(0, 2)
            keep_ids(0, src_f, 0, range(1, QUADS))
            act.wait_ge(s_b_first_kept, 2)
            act.dma_start(table_b[0:AHEAD * P, :].rearrange("(b p) f -> p b f", p=P), b_first[:, :, :]
                          ).then_inc(s_b_stored, 16)
            keep_ids(1, dst_f, QUADS, range(QUADS))

            act.wait_ge(s_planned, 1)
            crooked = act.value_load(flag[0:1, 0:1], min_val=0, max_val=ID_ROWS)

            act.wait_ge(s_norm, 1)

            def h_of(rows, b):
                return act.activation(rows, x_block(b), ACT.Relu, bias=shift_all[:, bass.ds(b, 1)],
                                      scale=scale_all[:, bass.ds(b, 1)])

            def stage(b):
                if past(b, 1):
                    act.wait_ge(s_fin_turned, b)
                    act.wait_ge(s_total, b)
                act.activation(staged[:, :], aggr[:, bass.ds(b * P, P)], ACT.Copy).then_inc(s_staged, 1)
                h_of(h_again[:, :], b).then_inc(s_h_again, 1)

            def deviate(b):
                act.wait_ge(s_o_var, b + 1)
                if past(b, 1):
                    act.wait_ge(s_o_vec, b * 5)
                act.activation(o_dev[:, :], o_moments[:, 1:2], ACT.Sqrt, bias=eps[:, 0:1]).then_inc(s_o_dev, 1)

            def h_ahead(j):
                if past(j, 1):
                    act.wait_ge(s_hb_turned, j)
                h_of(hb_rows[:, :], j + AHEAD).then_inc(s_hb, 1)

            def store_b(j):
                act.wait_ge(s_b_kept, j + 1)
                act.dma_start(table_b[bass.ds((j + AHEAD) * P, P), :], b_rows[:, :]).then_inc(s_b_stored, 16)

            with act.If(crooked < 1):
                def columns(i, u):
                    g = i * UNROLL + u
                    act.wait_ge(s_edge_turned, g + 1)
                    if past(g, 2):
                        act.wait_ge(s_pre, g - 1)
                    act.activation(edge_cols[:, u % 2, :], ps_edge[u % 2][:, :], ACT.Copy).then_inc(s_edge_cols, 1)
                    act.wait_ge(s_hot_turned, g + 1)
                    act.activation(onehot_cols[:, u % 2, :], ps_hot[u % 2][:, :], ACT.Copy).then_inc(s_hot_cols, 1)

                def relu(i, u):
                    act.wait_ge(s_z, i * UNROLL + u + 1)
                    act.activation(msg[:, u % 2, :, :], msg[:, u % 2, :, :], ACT.Relu).then_inc(s_msg, 1)

                def round_(i, groups=UNROLL):
                    last = groups < UNROLL
                    for u in range(groups):
                        if not (last and u == groups - 1):
                            columns(*after(i, u, 1))
                        if u == 3 and past(i, 2):
                            deviate(i - 2)
                        relu(i, u)
                        if u == 1:
                            if past(i, 2):
                                act.wait_ge(s_added, i * UNROLL)
                                stage(i - 2)
                            if not last:
                                h_ahead(i)
                                if past(i, 1):
                                    store_b(i - 1)

                columns(0, 0)
                for i in range(3):
                    round_(i)
                with act.Fori(3, ROUNDS - 1) as i:
                    round_(i)
                round_(ROUNDS - 1, LEFT)
                deviate(ROUNDS - 3)
                act.wait_ge(s_added, GROUPS)
                for b in (BLOCKS - 2, BLOCKS - 1):
                    stage(b)
                    deviate(b)
            with act.Else():
                h_ahead(0)
                store_b(0)
                with act.Fori(1, ROUNDS - 1) as j:
                    h_ahead(j)
                    store_b(j)
                with act.Fori(0, GROUPS) as g:
                    act.wait_ge(g_turned, g + 1)
                    act.activation(edge_cols[:, 0, :], ps_edge[0][:, :], ACT.Copy).then_inc(g_cols, 1)
                    act.wait_ge(g_z2, g + 1)
                    act.activation(msg[:, 0, :, :], msg[:, 0, :, :], ACT.Relu).then_inc(g_msg, 1)
                act.wait_ge(g_added, GROUPS * WIDES + 1)
                stage(0)
                deviate(0)
                with act.Fori(1, BLOCKS) as b:
                    stage(b)
                    deviate(b)

        @block.vector
        def _(dve):
            def moments(c, par, half):
                loads = 2 if isinstance(c, int) and c == CHUNKS - 2 else 1
                dve.wait_ge(s_x[par], (half + loads) * 16)
                if past(c, 2):
                    dve.wait_ge(s_var, c - 1)
                for k in range(CHUNK):
                    ins = dve.bn_stats(halves[:, par, k, :], x_block(first_block(c) + k))
                ins.then_inc(s_vec, 1)

            def pair_sums(c, par):
                dve.wait_ge(s_vec, c * 2 + 1)
                dve.tensor_tensor(pair_sum[:, par, :, :], halves[:, par, :, 1:3], halves[:, par, :, 4:6], ALU.add
                                  ).then_inc(s_vec, 1)

            def means(c, par):
                dve.wait_ge(s_vec, c * 2 + 2)
                dve.tensor_scalar(mean_all[:, bass.ds(first_block(c), CHUNK)], pair_sum[:, par, :, 0], 0.5, None,
                                  ALU.mult).then_inc(s_mean, 1)

            def scale(c):
                dve.wait_ge(s_dev, c + 1)
                dve.reciprocal(scale_all[:, bass.ds(first_block(c), CHUNK)], deviation[:, :]).then_inc(s_scale, 1)

            def keep_a(c, par, half):
                dve.wait_ge(s_scale, c + 1)
                dve.wait_ge(s_tab, c + 1)
                if past(half, 1):
                    dve.wait_ge(s_a_stored[par], half * 16)
                dve.tensor_tensor(a_out[:, par, 0:4, :], ps_tab[par][0][:, :].rearrange("p (b f) -> p b f", b=4),
                                  scale_all[:, bass.ds(first_block(c), 4)].unsqueeze(2).to_broadcast([P, 4, H]), ALU.mult
                                  ).then_inc(s_a_kept[0], 1)

            def step(c, par, half):
                moments(c + 2, par, half + 1)
                pair_sums(c + 2, par)
                if past(c, 1):
                    scale(c - 1)
                means(c + 2, par)
                if past(c, 1):
                    keep_a(c - 1, 1 - par, half - 1 + par)

            def pick(i, u):
                dve.tensor_copy(picks[:, u, :], src_f[:, bass.ds(i * UNROLL + u, 1), :].rearrange("p o k -> p (o k)")
                                ).then_inc(s_picks, 1)

            def extreme(to, q, op):
                return dve.tensor_reduce(to[0:ROWS, q:q + 1], ids_f[0:ROWS, 1, q, :], AX.X, op)

            for c in range(2):
                moments(c, c, 0)
                pair_sums(c, c)
                means(c, c)
            for c in range(4):
                step(c, c % 2, c // 2)
            with dve.Fori(2, CHUNKS // 2 - 2) as pair:
                for par in range(2):
                    step(pair * 2 + par, par, pair)
            for c in range(CHUNKS - 4, CHUNKS - 2):
                step(c, c % 2, c // 2)
            at = first_block(CHUNKS - 1) + 4
            dve.wait_ge(s_mean, CHUNKS)
            dve.tensor_tensor(centred[:, 1, 4:CHUNK, :], x_all[:, at:at + CHUNK - 4, :],
                              mean_all[:, at:at + CHUNK - 4].unsqueeze(2).to_broadcast([P, CHUNK - 4, H]),
                              ALU.subtract).then_inc(s_centred_last, 1)
            dve.wait_ge(s_cast[1], 1)
            for q in range(2):
                extreme(lowest, q, ALU.min)
            scale(CHUNKS - 3)
            scale(CHUNKS - 2)
            keep_a(CHUNKS - 3, 1, CHUNKS // 2 - 2)
            for q in range(2, QUADS):
                ins = extreme(lowest, q, ALU.min)
            ins.then_inc(s_range, 1)
            scale(CHUNKS - 1)
            keep_a(CHUNKS - 2, 0, CHUNKS // 2 - 1)
            for q in range(2):
                extreme(highest, q, ALU.max)
            keep_a(CHUNKS - 1, 1, CHUNKS // 2 - 1)
            for q in range(2, QUADS):
                ins = extreme(highest, q, ALU.max)
            ins.then_inc(s_range, 1)
            dve.wait_ge(s_const, 5)
            dve.wait_ge(s_range, 2)
            dve.tensor_tensor(highest[0:ROWS, :], highest[0:ROWS, :], lowest[0:ROWS, :], ALU.subtract
                              ).then_inc(s_range, 1)
            dve.tensor_tensor(even[0:ROWS, :], lowest[0:ROWS, :], even[0:ROWS, :], ALU.subtract
                              ).then_inc(s_range, 1)
            dve.wait_ge(s_range, 4)
            dve.tensor_scalar(highest[0:ROWS, :], highest[0:ROWS, :], float(WIN), None, ALU.is_ge
                              ).then_inc(s_range, 1)
            dve.tensor_tensor(even[0:ROWS, :], even[0:ROWS, :], even[0:ROWS, :], ALU.mult).then_inc(s_range, 1)
            dve.wait_ge(s_range, 6)
            dve.scalar_tensor_tensor(out=bad[0:ROWS, :], in0=even[0:ROWS, :], scalar=float(LEAD * LEAD),
                                     in1=highest[0:ROWS, :], op0=ALU.is_gt, op1=ALU.max).then_inc(s_bad, 1)
            dve.scalar_tensor_tensor(out=shift_all[:, 0:BLOCKS], in0=mean_all[:, :], scalar=-1.0,
                                     in1=scale_all[:, 0:BLOCKS], op0=ALU.mult, op1=ALU.mult).then_inc(s_norm, 1)
            dve.wait_ge(s_ids_kept, 1)
            for u in range(UNROLL):
                pick(0, u)
            dve.wait_ge(s_plan, 1)
            dve.tensor_copy(flag[:, :], ps_bad).then_inc(s_planned, 1)
            dve.tensor_copy(base_i[:, :], ps_base[0:1, 0:ID_ROWS]).then_inc(s_planned, 1)
            dve.tensor_copy(base_all[:, :], ps_base[:, 0:ID_ROWS]).then_inc(s_planned, 1)

            dve.wait_ge(s_planned, 3)
            crooked = dve.value_load(flag[0:1, 0:1], min_val=0, max_val=ID_ROWS)
            dve.wait_ge(s_zero, 1)

            def mask():
                dve.wait_ge(s_ids_kept, 2 * QUADS)
                dve.memset(dst_f[0:TAIL_DONE, FULL_GROUPS, :], -1.0).then_inc(s_rel, 1)
                dve.wait_ge(s_rel, 1)

            def hb_columns(j):
                dve.wait_ge(s_hb_turned, j + 1)
                if past(j, 1):
                    dve.wait_ge(s_b_tab, j)
                dve.tensor_copy(hb_cols[:, :], ps_hb).then_inc(s_hb_cols, 1)

            def keep_b(j):
                dve.wait_ge(s_b_tab, j + 1)
                dve.wait_ge(s_b_stored, (j + 1) * 16)
                dve.tensor_tensor(b_rows[:, :], ps_b, b1_all[:, :], ALU.add).then_inc(s_b_kept, 1)

            def add_h(b):
                dve.wait_ge(s_fin_turned, b + 1)
                dve.wait_ge(s_h_again, b + 1)
                if past(b, 1):
                    dve.wait_ge(s_o_vec, b * 5)
                dve.tensor_tensor(total[:, :], ps_total, h_again[:, :], ALU.add).then_inc(s_total, 1)
                dve.wait_ge(s_total, b + 1)
                dve.bn_stats(o_halves[:, :], total[:, :]).then_inc(s_o_vec, 1)
                dve.wait_ge(s_o_vec, b * 5 + 1)
                dve.sem_inc(s_gate_dve, 1)
                dve.bn_aggr(o_moments[:, :], o_halves[:, :]).then_inc(s_o_var, 1)

            def finish(b):
                dve.wait_ge(s_o_dev, b + 1)
                dve.reciprocal(o_scale[:, :], o_dev[:, :]).then_inc(s_o_vec, 1)
                if past(b, 1):
                    dve.wait_ge(s_out_stored, b * 16)
                dve.wait_ge(s_o_vec, b * 5 + 2)
                dve.tensor_scalar(out_rows[:, :], total[:, :], o_moments[:, 0:1], o_scale[:, 0:1],
                                  ALU.subtract, ALU.mult).then_inc(s_o_vec, 1)
                dve.wait_ge(s_o_vec, b * 5 + 3)
                dve.tensor_tensor(out_rows[:, :], out_rows[:, :], gamma_all[:, :], ALU.mult).then_inc(s_o_vec, 1)
                dve.wait_ge(s_o_vec, b * 5 + 4)
                dve.tensor_tensor(out_rows[:, :], out_rows[:, :], beta_all[:, :], ALU.add).then_inc(s_o_vec, 1)
                dve.wait_ge(s_o_vec, b * 5 + 5)
                dve.tensor_tensor(out_rows[:, :], out_rows[:, :], x_block(b), ALU.add).then_inc(s_out, 1)

            with dve.If(crooked < 1):
                def one_hot(i, u):
                    if past(i, 1):
                        dve.wait_ge(s_sum, (i - 1) * UNROLL + u + 1)
                    dve.tensor_tensor(
                        onehot[:, u, :, 0:WIN],
                        dst_f[:, bass.ds(i * UNROLL + u, 1), :].rearrange("p o k -> p (o k)").unsqueeze(2)
                        .to_broadcast([P, SUB, WIN]),
                        count[:, 0:WIN].unsqueeze(1).to_broadcast([P, SUB, WIN]),
                        ALU.is_equal).then_inc(s_hot, 1)

                def add_a(i, u):
                    g = i * UNROLL + u
                    dve.wait_ge(s_pre, g + 1)
                    for k in range(SUB):
                        dve.wait_ge(s_a_rows[u][k], (i + 1) * 16)
                    if past(g, 2):
                        dve.wait_ge(s_sum, g - 1)
                    dve.tensor_tensor(msg[:, u % 2, :, :].rearrange("p k f -> p (k f)"), ps_pre[u % 2][:, :],
                                      a_rows[:, u, :, :].rearrange("p k f -> p (k f)"), ALU.add).then_inc(s_z, 1)

                def add_sums(i, u):
                    g = i * UNROLL + u
                    base = dve.value_load(base_i[0:1, bass.ds(g, 1)], min_val=0, max_val=N - 1)
                    dve.wait_ge(s_sum, g + 1)
                    if past(g, 1):
                        dve.wait_ge(s_added, g)
                    at = aggr[:, bass.ds(base, WIN)]
                    dve.tensor_tensor(at, ps_sums[u % 2], at, ALU.add).then_inc(s_added, 1)

                def clear(j):
                    dve.tensor_copy(aggr[:, bass.ds((j + AHEAD) * P, P)], zeros[:, :])

                def round_(i, groups=UNROLL):
                    last = groups < UNROLL
                    for u in range(groups):
                        if not (last and u + 2 >= groups):
                            one_hot(*after(i, u, 2))
                        add_a(i, u)
                        if not last and not (isinstance(i, int) and i == ROUNDS - 2 and u >= LEFT):
                            pick(i + 1, u)
                        if past(i * UNROLL + u, 1):
                            add_sums(*before(i, u))
                        if u == 0 and past(i, 1):
                            clear(i - 1)
                            keep_b(i - 1)
                        if u == 2:
                            if past(i, 2):
                                add_h(i - 2)
                            if not last:
                                hb_columns(i)
                        if u == 3 and past(i, 2):
                            finish(i - 2)

                mask()
                dve.tensor_tensor(dst_f[:, :, :], dst_f[:, :, :],
                                  base_all[:, :].unsqueeze(2).to_broadcast([P, ID_ROWS, SUB]),
                                  ALU.subtract).then_inc(s_rel, 1)
                dve.memset(aggr[:, 0:AHEAD * P], 0.0)
                dve.wait_ge(s_rel, 2)
                one_hot(0, 0)
                one_hot(0, 1)
                for i in range(3):
                    round_(i)
                with dve.Fori(3, ROUNDS - 1) as i:
                    round_(i)
                round_(ROUNDS - 1, LEFT)
                finish(ROUNDS - 3)
                add_sums(ROUNDS - 1, LEFT - 1)
                for b in (BLOCKS - 2, BLOCKS - 1):
                    add_h(b)
                    finish(b)
            with dve.Else():
                mask()
                dve.memset(aggr[:, :], 0.0).then_inc(g_added, 1)
                dve.wait_ge(g_added, 1)
                hb_columns(0)
                keep_b(0)
                with dve.Fori(1, ROUNDS - 1) as j:
                    hb_columns(j)
                    keep_b(j)
                with dve.Fori(0, GROUPS) as g:
                    senders = src_f[:, bass.ds(g, 1), :].rearrange("p o k -> p (o k)")
                    receivers = dst_f[:, bass.ds(g, 1), :].rearrange("p o k -> p (o k)")
                    dve.tensor_copy(picks[:, 0, :], senders).then_inc(g_picks, 1)
                    dve.tensor_scalar(picks[:, 1, :], receivers, 0.0, None, ALU.max).then_inc(g_picks, 1)
                    dve.wait_ge(g_pre, g + 1)
                    for k in range(2 * SUB):
                        dve.wait_ge(g_rows[k], (g + 1) * 16)
                    z = msg[:, 0, :, :].rearrange("p k f -> p (k f)")
                    dve.tensor_tensor(z, ps_pre[0][:, :], a_rows[:, 0, :, :].rearrange("p k f -> p (k f)"),
                                      ALU.add).then_inc(g_z, 1)
                    dve.wait_ge(g_z, g + 1)
                    dve.tensor_tensor(z, z, a_rows[:, 1, :, :].rearrange("p k f -> p (k f)"), ALU.add
                                      ).then_inc(g_z2, 1)
                    with dve.Fori(0, WIDES) as w:
                        for k in range(SUB):
                            ins = dve.tensor_scalar(onehot[:, k, :, :].rearrange("p k n -> p (k n)"), count[:, :],
                                                    receivers[:, k:k + 1], None, ALU.is_equal)
                        ins.then_inc(g_hot, 1)
                        dve.wait_ge(g_hot, g * WIDES + w + 1)
                        dve.tensor_scalar(receivers, receivers, -float(WIDE), None, ALU.add).then_inc(g_rel, 1)
                        dve.wait_ge(g_sum, g * WIDES + w + 1)
                        at = aggr[:, bass.ds(w * WIDE, WIDE)]
                        dve.tensor_tensor(at, ps_sum[:, :], at, ALU.add).then_inc(g_added, 1)
                        dve.wait_ge(g_added, g * WIDES + w + 2)
                        dve.wait_ge(g_rel, g * WIDES + w + 1)
                add_h(0)
                finish(0)
                with dve.Fori(1, BLOCKS) as b:
                    add_h(b)
                    finish(b)


_INS = ["x", "src", "dst", "edge_attr_128", "L0_gnn_W1", "L0_gnn_b1", "L0_gnn_ln_gamma", "L0_gnn_ln_beta"]


def kernel(**inputs):
    import numpy as _np
    import concourse.bacc as _bacc
    from concourse import mybir as _mybir
    from concourse.bass_utils import run_bass_kernel_spmd as _run

    nc = _bacc.Bacc("TRN2", target_bir_lowering=False, num_devices=1)
    arrays, args = {}, []
    for name in _INS:
        a = _np.ascontiguousarray(inputs[name])
        arrays[f"in_{name}"] = a
        args.append(nc.dram_tensor(f"in_{name}", a.shape, _mybir.dt.from_np(a.dtype), kind="ExternalInput").ap())
    shape = inputs["x"].shape
    args.append(nc.dram_tensor("out_0", shape, _mybir.dt.float32, kind="ExternalOutput").ap())
    build(nc, *args)
    r = _run(nc, [arrays], core_ids=[0])
    return r.results[0]["out_0"]
```

```python
from contextlib import ExitStack

import concourse.bass as bass
from concourse import mybir

F32 = mybir.dt.float32
I32 = mybir.dt.int32
ALU = mybir.AluOpType
ACT = mybir.ActivationFunctionType
AX = mybir.AxisListType

P = 128
H = 128
EPS = 1e-5
SUB = 4
GROUP = P * SUB
UNROLL = 4
WIN = 64
LEAD = 128
X_LEAD = 4
EARLY = 8
AHEAD = 5
WIDE = 512
CHUNK = 7
SHARED = 3


def past(value, n):
    return not isinstance(value, int) or value >= n


def build(nc, x, src, dst, edge_attr, w1, b1, gamma, beta, out):
    N, E = x.shape[0], edge_attr.shape[0]
    BLOCKS = -(-N // P)
    LAST_ROWS = N - (BLOCKS - 1) * P
    FULL_GROUPS = E // GROUP
    GROUPS = -(-E // GROUP)
    ROUNDS = -(-GROUPS // UNROLL)
    TAIL_START = E - GROUP
    TAIL_DONE = (FULL_GROUPS * GROUP - TAIL_START) // SUB
    QUADS = 4
    ROWS = -(-GROUPS // QUADS)
    ID_ROWS = QUADS * ROWS
    PER_GROUP = P // UNROLL
    CHUNKS = BLOCKS // CHUNK
    ALL_BLOCKS = ROUNDS - 1 + AHEAD
    WIDES = -(-(BLOCKS * P) // WIDE)
    ID_LOADS = 2 + ROWS - (FULL_GROUPS - (QUADS - 1) * ROWS)
    EARLY_GROUPS = (ROUNDS - 1) // EARLY
    EARLY_ROWS = EARLY_GROUPS * SUB
    EARLY_AT = AHEAD + 3
    LEFT = GROUPS - (ROUNDS - 1) * UNROLL
    assert BLOCKS == ROUNDS and CHUNKS % 2 == 0 and CHUNKS * CHUNK == BLOCKS and CHUNKS >= 6
    assert E % SUB == 0 and FULL_GROUPS == GROUPS - 1 and ID_ROWS == GROUPS + 1 and ROWS <= P
    assert EARLY_GROUPS * EARLY == ROUNDS - 2 and 3 + SUB < EARLY and EARLY_ROWS % EARLY == 0
    assert EARLY_AT + EARLY_ROWS <= ALL_BLOCKS - 2 * QUADS * SUB
    assert LEFT == 3 and WIDES * WIDE <= ALL_BLOCKS * P and AHEAD <= CHUNK
    assert PER_GROUP * (UNROLL - 1) + LEAD + WIN <= 3 * P

    table_a = nc.dram_tensor("table_a", (BLOCKS * P, H), F32)
    table_early = nc.dram_tensor("table_early", (EARLY_ROWS * P, H), F32)
    table_b = nc.dram_tensor("table_b", (ALL_BLOCKS * P, H), F32)

    ctx = ExitStack()
    with ctx:
        def sb(name, shape, dt=F32):
            return ctx.enter_context(nc.sbuf_tensor(name, shape, dt))

        def bank(name):
            return ctx.enter_context(nc.psum_tensor(name, [P, 512], F32))

        def sem(name):
            return ctx.enter_context(nc.semaphore(name))

        x_all = sb("x_all", [P, ALL_BLOCKS, H])
        aggr = sb("aggr", [P, ALL_BLOCKS * P])
        src_f = sb("src_f", [P, ID_ROWS, SUB])
        dst_f = sb("dst_f", [P, ID_ROWS, SUB])
        base_all = sb("base_all", [P, ID_ROWS])
        base_i = sb("base_i", [1, ID_ROWS], I32)
        scale_all = sb("scale_all", [P, ALL_BLOCKS])
        shift_all = sb("shift_all", [P, ALL_BLOCKS])
        ident = sb("ident", [P, P])
        ones = sb("ones", [P, P])
        zeros = sb("zeros", [P, P])
        eps = sb("eps", [P, 1])
        count = sb("count", [P, WIDE])
        w_a = sb("w_a", [P, H])
        w_b = sb("w_b", [P, H])
        w_c = sb("w_c", [P, H])
        b1_all = sb("b1_all", [P, H])
        gamma_all = sb("gamma_all", [P, H])
        beta_all = sb("beta_all", [P, H])
        flag = sb("flag", [1, 1], I32)
        centred = sb("centred", [P, 2, CHUNK, H])
        mean_all = sb("mean_all", [P, BLOCKS])
        h_cols = sb("h_cols", [P, 2, CHUNK, P])
        a_out = sb("a_out", [P, 2, CHUNK, H])
        b_first = sb("b_first", [P, AHEAD, H])
        halves = sb("halves", [P, CHUNK, 6])
        pair_sum = sb("pair_sum", [P, CHUNK, 2])
        pair_gap = sb("pair_gap", [P, CHUNK])
        gap_sq = sb("gap_sq", [P, CHUNK])
        four_var = sb("four_var", [P, CHUNK])
        deviation = sb("deviation", [P, CHUNK])
        ids_at = ALL_BLOCKS * P - 2 * QUADS * GROUP
        ids_f = aggr[:, ids_at:].rearrange("p (a q e) -> p a q e", a=2, q=QUADS)
        ids_i = aggr[:, ids_at:].bitcast(I32).rearrange("p (a q e) -> p a q e", a=2, q=QUADS)
        lowest = sb("lowest", [P, QUADS])
        highest = sb("highest", [P, QUADS])
        even = sb("even", [P, QUADS])
        bad = sb("bad", [P, QUADS])
        diagonal = sb("diagonal", [P, QUADS, P])
        edges = sb("edges", [P, UNROLL, GROUP])
        a_rows = sb("a_rows", [P, UNROLL, SUB, H])
        b_win = sb("b_win", [P, UNROLL, H])
        picks = sb("picks", [P, UNROLL, SUB], I32)
        onehot = sb("onehot", [P, 4, SUB, P])
        edge_cols = sb("edge_cols", [P, 2, GROUP])
        onehot_cols = sb("onehot_cols", [P, 2, GROUP])
        msg = sb("msg", [P, 2, SUB, H])
        hb_rows = sb("hb_rows", [P, H])
        hb_cols = sb("hb_cols", [P, P])
        b_rows = sb("b_rows", [P, H])
        early_picks = sb("early_picks", [P, EARLY_GROUPS, SUB], I32)
        e_halves = sb("e_halves", [P, 6])
        e_moments = sb("e_moments", [P, 2])
        e_dev = sb("e_dev", [P, 1])
        e_scale = sb("e_scale", [P, 1])
        e_norm = sb("e_norm", [P, H])
        e_cols = sb("e_cols", [P, P])
        e_rows = sb("e_rows", [P, H])
        staged = sb("staged", [P, 2, P])
        h_again = sb("h_again", [P, 2, H])
        total = sb("total", [P, 2, H])
        x_beta = sb("x_beta", [P, 2, H])
        scaled = sb("scaled", [P, 2, H])
        out_rows = sb("out_rows", [P, 2, H])
        o_halves = sb("o_halves", [P, 2, 6])
        o_moments = sb("o_moments", [P, 2, 2])
        o_dev = sb("o_dev", [P, 2])
        o_scale = sb("o_scale", [P, 2])

        ps_edge = [bank("ps_edge0"), bank("ps_edge1")]
        ps_hot = [bank("ps_hot0"), bank("ps_hot1")]
        ps_pre = [bank("ps_pre0"), bank("ps_pre1")]
        ps_sum = bank("ps_sum")
        ps_fin = bank("ps_fin")
        ps_sums = [ps_sum[:, 0:WIN], ps_fin[:, P:P + WIN]]
        ps_total = [ps_fin[:, 0:P], ps_edge[0][:, 0:P]]
        ps_hb, ps_b = ps_fin[:, 2 * P:3 * P], ps_fin[:, 3 * P:4 * P]
        ps_early, ps_early_a = ps_sum[:, P:2 * P], ps_sum[:, 2 * P:3 * P]
        ps_turn = [[ps_edge[0], ps_edge[1]], [ps_hot[0], ps_hot[1]]]
        ps_tab = [[ps_pre[0], ps_pre[1]], [ps_sum, ps_fin]]
        ps_first = ps_hot
        ps_base, ps_bad = ps_edge[0], ps_edge[1][0:1, 0:1]
        ps_ids = [[ps_pre[0], ps_pre[1], ps_sum, ps_fin], [ps_hot[0], ps_hot[1], ps_edge[0], ps_edge[1]]]

        s_w_a = sem("s_w_a")
        s_weights = sem("s_weights")
        s_ids = [sem("s_ids_src"), sem("s_ids_dst")]
        s_x = [sem("s_x0"), sem("s_x1")]
        s_pad = sem("s_pad")
        s_const = sem("s_const")
        s_cast = [sem("s_cast_src"), sem("s_cast_dst")]
        s_range = sem("s_range")
        s_diag = sem("s_diag")
        s_bad = sem("s_bad")
        s_ids_turned = sem("s_ids_turned")
        s_ids_kept = sem("s_ids_kept")
        s_plan = sem("s_plan")
        s_planned = sem("s_planned")
        s_vec = sem("s_vec")
        s_var = sem("s_var")
        s_dev = sem("s_dev")
        s_mean = sem("s_mean")
        s_scale = sem("s_scale")
        s_norm = sem("s_norm")
        s_centred = sem("s_centred")
        s_turned = sem("s_turned")
        s_h_cols = sem("s_h_cols")
        s_tab = sem("s_tab")
        s_a_kept = [sem("s_a_kept_dve"), sem("s_a_kept_act")]
        s_a_stored = [sem("s_a_stored0"), sem("s_a_stored1")]
        s_b_first = sem("s_b_first")
        s_b_first_kept = sem("s_b_first_kept")
        s_b_stored = sem("s_b_stored")
        s_zero = sem("s_zero")
        s_gate_pool = sem("s_gate_pool")
        s_gate_dve = sem("s_gate_dve")
        s_edges = [sem(f"s_edges{u}") for u in range(UNROLL)]
        s_b_win = [sem(f"s_b_win{u}") for u in range(UNROLL)]
        s_a_rows = [[sem(f"s_a_rows{u}_{k}") for k in range(SUB)] for u in range(UNROLL)]
        s_picks = sem("s_picks")
        s_rel = sem("s_rel")
        s_hot = sem("s_hot")
        s_edge_turned = sem("s_edge_turned")
        s_hot_turned = sem("s_hot_turned")
        s_edge_cols = sem("s_edge_cols")
        s_hot_cols = sem("s_hot_cols")
        s_pre = sem("s_pre")
        s_z = sem("s_z")
        s_msg = sem("s_msg")
        s_sum = sem("s_sum")
        s_added = sem("s_added")
        s_hb = sem("s_hb")
        s_hb_turned = sem("s_hb_turned")
        s_hb_cols = sem("s_hb_cols")
        s_b_tab = sem("s_b_tab")
        s_b_kept = sem("s_b_kept")
        s_staged = sem("s_staged")
        s_h_again = sem("s_h_again")
        s_fin_turned = sem("s_fin_turned")
        s_total = sem("s_total")
        s_x_beta = sem("s_x_beta")
        s_o_halves = sem("s_o_halves")
        s_o_moments = sem("s_o_moments")
        s_scaled = sem("s_scaled")
        s_o_dev = sem("s_o_dev")
        s_o_scale = sem("s_o_scale")
        s_out = sem("s_out")
        s_out_stored = sem("s_out_stored")
        s_early_picks = sem("s_early_picks")
        s_early_raw = sem("s_early_raw")
        s_e_halves = sem("s_e_halves")
        s_e_moments = sem("s_e_moments")
        s_e_dev = sem("s_e_dev")
        s_e_scale = sem("s_e_scale")
        s_e_norm = sem("s_e_norm")
        s_e_turned = sem("s_e_turned")
        s_e_cols = sem("s_e_cols")
        s_e_a = sem("s_e_a")
        s_e_rows = sem("s_e_rows")
        s_e_stored = sem("s_e_stored")
        s_early_loaded = sem("s_early_loaded")
        g_edges = sem("g_edges")
        g_picks = sem("g_picks")
        g_rows = [sem(f"g_rows{k}") for k in range(2 * SUB)]
        g_turned = sem("g_turned")
        g_cols = sem("g_cols")
        g_pre = sem("g_pre")
        g_z = sem("g_z")
        g_z2 = sem("g_z2")
        g_msg = sem("g_msg")
        g_hot = sem("g_hot")
        g_rel = sem("g_rel")
        g_sum = sem("g_sum")
        g_added = sem("g_added")

        block = ctx.enter_context(nc.Block())

        def first_block(c):
            return 0 if isinstance(c, int) and c == CHUNKS - 1 else c * CHUNK + CHUNK

        def node_rows(tensor, c):
            return tensor[bass.ds(first_block(c) * P, CHUNK * P), :].rearrange("(b p) f -> p b f", p=P)

        def a_tile(c, par):
            return centred[:, 0, :, :] if isinstance(c, int) and c == CHUNKS - 1 else a_out[:, par, :, :]

        def group_rows(start):
            return edge_attr[bass.ds(start, GROUP), :].rearrange("(p k) f -> p (k f)", p=P)

        def start_of(i, u):
            if isinstance(i, int) and i * UNROLL + u >= FULL_GROUPS:
                return TAIL_START
            return i * (UNROLL * GROUP) + u * GROUP

        def x_block(b):
            return x_all[:, bass.ds(b, 1), :].rearrange("p o f -> p (o f)")

        def before(i, u):
            return (i, u - 1) if u else (i - 1, UNROLL - 1)

        def after(i, u, n):
            return (i, u + n) if u + n < UNROLL else (i + 1, u + n - UNROLL)


        @block.sync
        def _(sp):
            def load_x(c, par):
                if not isinstance(c, int) or c != CHUNKS - 2:
                    sp.dma_start(x_all[:, bass.ds(first_block(c), CHUNK), :], node_rows(x, c)).then_inc(s_x[par], 16)
                else:
                    first = first_block(c)
                    sp.dma_start(x_all[:, first:BLOCKS - 1, :],
                                 x[first * P:(BLOCKS - 1) * P, :].rearrange("(b p) f -> p b f", p=P)
                                 ).then_inc(s_x[par], 16)
                    sp.wait_ge(s_pad, 1)
                    sp.dma_start(x_all[0:LAST_ROWS, BLOCKS - 1, :], x[(BLOCKS - 1) * P:N, :]
                                 ).then_inc(s_x[par], 16)

            def load_ids(a, ids):
                full = FULL_GROUPS - (QUADS - 1) * ROWS
                sp.dma_start(ids_i[0:ROWS, a, 0:QUADS - 1, :],
                             ids[0:(QUADS - 1) * ROWS * GROUP].rearrange("(q r e) -> r q e", q=QUADS - 1, r=ROWS)
                             ).then_inc(s_ids[a], 16)
                sp.dma_start(ids_i[0:full, a, QUADS - 1, :],
                             ids[(QUADS - 1) * ROWS * GROUP:FULL_GROUPS * GROUP].rearrange("(r e) -> r e", r=full)
                             ).then_inc(s_ids[a], 16)
                for r in range(full, ROWS):
                    sp.dma_start(ids_i[r:r + 1, a, QUADS - 1, :],
                                 ids[TAIL_START:E].rearrange("(r e) -> r e", r=1)).then_inc(s_ids[a], 16)

            def next_x(pair, par):
                sp.wait_ge(s_x[par], pair * 16)
                load_x(pair * 2 + par, par)

            def store_a(pair, par):
                c = pair * 2 + par
                sp.wait_ge(s_a_kept[1], c + 1)
                if isinstance(c, int) and c >= CHUNKS - SHARED:
                    sp.wait_ge(s_a_kept[0], c - CHUNKS + SHARED + 1)
                sp.dma_start(node_rows(table_a, c), a_tile(c, par)).then_inc(s_a_stored[par], 16)

            load_x(0, 0)
            sp.dma_start(early_picks[:, :, :],
                         src[0:EARLY_GROUPS * EARLY * UNROLL * GROUP].rearrange(
                             "(s g p k) -> p s g k", s=EARLY_GROUPS, g=EARLY * UNROLL, p=P)[:, :, EARLY * UNROLL - 1, :]
                         ).then_inc(s_early_picks, 16)
            load_x(1, 1)
            sp.dma_start(w_a[:, :], w1[0:H, :]).then_inc(s_w_a, 16)
            load_ids(1, dst)
            next_x(1, 0)
            next_x(1, 1)
            sp.dma_start(w_b[:, :], w1[H:2 * H, :]).then_inc(s_weights, 16)
            sp.dma_start(w_c[:, :], w1[2 * H:3 * H, :]).then_inc(s_weights, 16)
            for tile, row in ((b1_all, b1), (gamma_all, gamma), (beta_all, beta)):
                sp.dma_start(tile[:, :], row.rearrange("(o f) -> o f", o=1).to_broadcast([P, H])
                             ).then_inc(s_weights, 16)
            for pair in range(2, X_LEAD):
                for par in range(2):
                    next_x(pair, par)
            load_ids(0, src)
            with sp.Fori(0, CHUNKS // 2 - 1 - X_LEAD) as pair:
                for par in range(2):
                    store_a(pair, par)
                    next_x(pair + X_LEAD, par)
            for par in range(2):
                store_a(CHUNKS // 2 - 1 - X_LEAD, par)
                next_x(CHUNKS // 2 - 1, par)
            with sp.Fori(CHUNKS // 2 - X_LEAD, CHUNKS // 2 - 2) as pair:
                for par in range(2):
                    store_a(pair, par)
            for c in range(CHUNKS - 4, CHUNKS):
                store_a(c // 2, c % 2)

            sp.wait_ge(s_planned, 2)
            crooked = sp.value_load(flag[0:1, 0:1], min_val=0, max_val=ID_ROWS)

            with sp.If(crooked < 1):
                def step(i, u):
                    g = i * UNROLL + u
                    if past(i, 1):
                        sp.wait_ge(s_edge_turned, g - UNROLL + 1)
                    sp.dma_start(edges[:, u, :], group_rows(start_of(i, u))).then_inc(s_edges[u], 16)
                    if past(i, 1):
                        sp.wait_ge(s_pre, g - UNROLL + 1)
                    if u == 0:
                        sp.wait_ge(s_b_stored, 16 if isinstance(i, int) and i < 2 else (i - 1) * 16)
                    base = sp.value_load(base_i[0:1, bass.ds(g, 1)], min_val=0, max_val=N - 1)
                    sp.dma_start(b_win[0:WIN, u, :], table_b[bass.ds(base, WIN), :]).then_inc(s_b_win[u], 16)

                sp.wait_ge(s_zero, 1)
                for i in range(3):
                    for u in range(UNROLL):
                        step(i, u)

                def round_(i):
                    for u in range(UNROLL):
                        step(i, u)
                    sp.wait_ge(s_out, i - 2)
                    sp.dma_start(out[bass.ds((i - 3) * P, P), :], out_rows[:, 0, :]).then_inc(s_out_stored, 16)

                def load_early(s):
                    i = s * EARLY + EARLY - 1
                    sp.wait_ge(s_e_stored, (s * SUB + SUB) * 16)
                    sp.wait_ge(s_z, i * UNROLL)
                    sp.dma_start(a_rows[:, UNROLL - 1, :, :],
                                 table_early[bass.ds(s * (SUB * P), SUB * P), :].rearrange("(k p) f -> p k f", p=P)
                                 ).then_inc(s_early_loaded, 16)

                with sp.Fori(3, EARLY) as i:
                    round_(i)
                load_early(0)
                with sp.Fori(1, EARLY_GROUPS) as s:
                    with sp.Fori(0, EARLY) as j:
                        round_(s * EARLY + j)
                    load_early(s)
                round_(ROUNDS - 2)
                for u in range(LEFT):
                    step(ROUNDS - 1, u)
                for b in range(ROUNDS - 4, BLOCKS):
                    rows = P if b < BLOCKS - 1 else LAST_ROWS
                    sp.wait_ge(s_out, b + 1)
                    sp.dma_start(out[b * P:b * P + rows, :], out_rows[0:rows, int(b == BLOCKS - 1), :]
                                 ).then_inc(s_out_stored, 16)
                sp.wait_ge(s_b_stored, (ROUNDS - 1) * 16)
                sp.wait_ge(s_out_stored, BLOCKS * 16)
            with sp.Else():
                def load(g, start):
                    if past(g, 1):
                        sp.wait_ge(g_turned, g)
                    sp.dma_start(edges[:, 0, :], group_rows(start)).then_inc(g_edges, 16)

                load(0, 0)
                with sp.Fori(1, FULL_GROUPS) as g:
                    load(g, g * GROUP)
                load(FULL_GROUPS, TAIL_START)
                with sp.Fori(0, BLOCKS - 1) as b:
                    sp.wait_ge(s_out, b + 1)
                    sp.dma_start(out[bass.ds(b * P, P), :], out_rows[:, 0, :]).then_inc(s_out_stored, 16)
                sp.wait_ge(s_out, BLOCKS)
                sp.dma_start(out[(BLOCKS - 1) * P:N, :], out_rows[0:LAST_ROWS, 0, :]).then_inc(s_out_stored, 16)
                sp.wait_ge(s_out_stored, BLOCKS * 16)

        @block.gpsimd
        def _(pool):
            pool.memset(ident[:, :], 0.0).then_inc(s_const, 1)
            pool.memset(ones[:, :], 1.0).then_inc(s_const, 1)
            pool.iota(even[:, :], pattern=[[ROWS * PER_GROUP, QUADS]], base=0, channel_multiplier=PER_GROUP,
                      allow_small_or_imprecise_dtypes=True).then_inc(s_const, 1)
            pool.memset(eps[:, :], EPS).then_inc(s_const, 1)
            pool.wait_ge(s_const, 4)
            pool.affine_select(out=ident[:, :], in_=ident[:, :], compare_op=ALU.not_equal, fill=1.0,
                               base=0, pattern=[[-1, P]], channel_multiplier=1).then_inc(s_const, 1)
            pool.memset(x_all[:, BLOCKS - 1:ALL_BLOCKS, :], 0.0).then_inc(s_pad, 1)
            pool.iota(count[:, :], pattern=[[1, WIDE]], base=0, channel_multiplier=0,
                      allow_small_or_imprecise_dtypes=True).then_inc(s_pad, 1)

            def gather_early(s):
                for k in range(SUB):
                    at = (EARLY_AT + s * SUB + k) * P
                    pool.indirect_dma_start(
                        aggr[:, at:at + P], None, x[:, :],
                        bass.IndirectOffsetOnAxis(ap=early_picks[:, s, k:k + 1], axis=0),
                    ).then_inc(s_early_raw, 16)

            pool.wait_ge(s_early_picks, 16)
            pool.sem_inc(s_gate_pool, 1)
            for s in range(EARLY_GROUPS - 3):
                gather_early(s)
            pool.wait_ge(s_ids[0], ID_LOADS * 16)
            for q in range(2):
                pool.tensor_copy(ids_f[0:ROWS, 0, q, :], ids_i[0:ROWS, 0, q, :]).then_inc(s_cast[0], 1)
            for s in range(EARLY_GROUPS - 3, EARLY_GROUPS):
                gather_early(s)
            pool.wait_ge(s_range, 1)
            pool.tensor_tensor(diagonal[0:ROWS, :, 0:ROWS],
                               ident[0:ROWS, 0:ROWS].unsqueeze(1).to_broadcast([ROWS, QUADS, ROWS]),
                               lowest[0:ROWS, :].unsqueeze(2).to_broadcast([ROWS, QUADS, ROWS]), ALU.mult
                               ).then_inc(s_diag, 1)
            pool.wait_ge(s_b_first_kept, 1)
            pool.wait_ge(s_weights, 80)
            pool.tensor_tensor(b_first[:, :, :], b_first[:, :, :],
                               b1_all[:, :].unsqueeze(1).to_broadcast([P, AHEAD, H]), ALU.add
                               ).then_inc(s_b_first_kept, 1)

            pool.wait_ge(s_planned, 1)
            crooked = pool.value_load(flag[0:1, 0:1], min_val=0, max_val=ID_ROWS)
            for par in range(2):
                pool.wait_ge(s_a_stored[par], (CHUNKS // 2) * 16)

            with pool.If(crooked < 1):
                def step(i, u):
                    pool.wait_ge(s_picks, i * UNROLL + u + 1)
                    if past(i, 1):
                        pool.wait_ge(s_z, (i - 1) * UNROLL + u + 1)
                    pool.sem_inc(s_gate_pool, 1)
                    for k in range(SUB):
                        pool.indirect_dma_start(
                            a_rows[:, u, k, :], None, table_a[:, :],
                            bass.IndirectOffsetOnAxis(ap=picks[:, u, k:k + 1], axis=0),
                        ).then_inc(s_a_rows[u][k], 16)

                def rounds(s, first):
                    with pool.Fori(first, EARLY - 1) as j:
                        for u in range(UNROLL):
                            step(s * EARLY + j, u)
                    for u in range(UNROLL - 1):
                        step(s * EARLY + EARLY - 1, u)

                for u in range(UNROLL):
                    step(0, u)
                rounds(0, 1)
                with pool.Fori(1, EARLY_GROUPS) as s:
                    rounds(s, 0)
                for u in range(UNROLL):
                    step(ROUNDS - 2, u)
                for u in range(LEFT):
                    step(ROUNDS - 1, u)
            with pool.Else():
                pool.wait_ge(s_b_stored, ROUNDS * 16)
                with pool.Fori(0, GROUPS) as g:
                    pool.wait_ge(g_picks, (g + 1) * 2)
                    pool.sem_inc(s_gate_pool, 1)
                    for k in range(SUB):
                        pool.indirect_dma_start(
                            a_rows[:, 0, k, :], None, table_a[:, :],
                            bass.IndirectOffsetOnAxis(ap=picks[:, 0, k:k + 1], axis=0),
                        ).then_inc(g_rows[k], 16)
                        pool.indirect_dma_start(
                            a_rows[:, 1, k, :], None, table_b[:, :],
                            bass.IndirectOffsetOnAxis(ap=picks[:, 1, k:k + 1], axis=0),
                        ).then_inc(g_rows[SUB + k], 16)
                    pool.wait_ge(g_z2, g + 1)

        @block.tensor
        def _(pe):
            pe.wait_ge(s_const, 5)

            def turn_ids(a, q):
                for k in range(SUB):
                    mm = pe.transpose(ps_ids[a][q][:, k * ROWS:(k + 1) * ROWS],
                                      ids_f[0:ROWS, a, q, k::SUB], ident[0:ROWS, 0:ROWS])
                mm.then_inc(s_ids_turned, 1)

            def turn_chunk(c, par):
                pe.wait_ge(s_centred, c + 1)
                if past(c, 2):
                    pe.wait_ge(s_h_cols, c - 1)
                for k in range(CHUNK):
                    mm = pe.transpose(ps_turn[par][k // 4][:, (k % 4) * P:(k % 4 + 1) * P],
                                      centred[:, par, k, :], ident[:, :])
                mm.then_inc(s_turned, 1)

            def table_chunk(c, par):
                pe.wait_ge(s_h_cols, c + 1)
                if past(c, 2):
                    pe.wait_ge(s_a_kept[1], c - 1)
                if isinstance(c, int) and c - 2 >= CHUNKS - SHARED:
                    pe.wait_ge(s_a_kept[0], c - 1 - CHUNKS + SHARED)
                for k in range(CHUNK):
                    mm = pe.matmul(ps_tab[par][k // 4][:, (k % 4) * H:(k % 4 + 1) * H],
                                   h_cols[:, par, k, :], w_a[:, :], start=True, stop=True)
                mm.then_inc(s_tab, 1)

            turn_chunk(0, 0)
            pe.wait_ge(s_w_a, 16)
            for c in range(1, 4):
                turn_chunk(c, c % 2)
                table_chunk(c - 1, (c - 1) % 2)
            pe.wait_ge(s_weights, 80)
            with pe.Fori(2, CHUNKS // 2 - 1) as pair:
                for par in range(2):
                    turn_chunk(pair * 2 + par, par)
                    table_chunk(pair * 2 + par - 1, 1 - par)
            for c in range(CHUNKS - 2, CHUNKS):
                turn_chunk(c, c % 2)
                table_chunk(c - 1, (c - 1) % 2)
            table_chunk(CHUNKS - 1, 1)
            for k in range(AHEAD):
                mm = pe.matmul(ps_first[k // 4][:, (k % 4) * H:(k % 4 + 1) * H],
                               h_cols[:, 1, k, :], w_b[:, :], start=True, stop=True)
            mm.then_inc(s_b_first, 1)
            pe.wait_ge(s_cast[0], 1)
            for a in range(2):
                pe.wait_ge(s_a_kept[a], (SHARED, CHUNKS)[a] - 1)
            turn_ids(0, 0)
            pe.wait_ge(s_diag, 1)
            for q in range(QUADS):
                pe.matmul(ps_base[:, q * ROWS:(q + 1) * ROWS], ones[0:ROWS, :], diagonal[0:ROWS, q, 0:ROWS],
                          start=True, stop=True)
            pe.wait_ge(s_bad, 1)
            for q in range(QUADS):
                mm = pe.matmul(ps_bad, bad[0:ROWS, q:q + 1], ones[0:ROWS, 0:1],
                               start=(q == 0), stop=(q == QUADS - 1))
            mm.then_inc(s_plan, 1)
            pe.wait_ge(s_cast[0], 3)
            turn_ids(0, 1)
            for a in range(2):
                pe.wait_ge(s_a_kept[a], (SHARED, CHUNKS)[a])
            turn_ids(0, 2)
            turn_ids(0, 3)
            pe.wait_ge(s_b_first_kept, 1)
            pe.wait_ge(s_cast[1], 1)
            turn_ids(1, 0)
            turn_ids(1, 1)
            pe.wait_ge(s_planned, 3)
            turn_ids(1, 2)
            turn_ids(1, 3)

            pe.wait_ge(s_planned, 1)
            crooked = pe.value_load(flag[0:1, 0:1], min_val=0, max_val=ID_ROWS)
            pe.wait_ge(s_ids_kept, 2 * QUADS)

            def turn_total(b, place=0):
                pe.wait_ge(s_staged, b + 1)
                if place == 0 and past(b, 1):
                    pe.wait_ge(s_total, b)
                pe.transpose(ps_total[place], staged[:, place, :], ident[:, :]).then_inc(s_fin_turned, 1)

            def turn_hb(j):
                pe.wait_ge(s_hb, j + 1)
                if past(j, 1):
                    pe.wait_ge(s_b_kept, j)
                pe.transpose(ps_hb, hb_rows[:, :], ident[:, :]).then_inc(s_hb_turned, 1)

            def table_b_block(j):
                pe.wait_ge(s_hb_cols, j + 1)
                pe.matmul(ps_b, hb_cols[:, :], w_b[:, :], start=True, stop=True).then_inc(s_b_tab, 1)

            with pe.If(crooked < 1):
                def turn(i, u):
                    g = i * UNROLL + u
                    pe.wait_ge(s_edges[u], (i + 1) * 16)
                    if past(g, 2):
                        pe.wait_ge(s_edge_cols, g - 1)
                    for k in range(SUB):
                        mm = pe.transpose(ps_edge[u % 2][:, k * P:(k + 1) * P],
                                          edges[:, u, k * H:(k + 1) * H], ident[:, :])
                    mm.then_inc(s_edge_turned, 1)
                    pe.wait_ge(s_hot, g + 1)
                    if past(g, 2):
                        pe.wait_ge(s_hot_cols, g - 1)
                    for k in range(SUB):
                        mm = pe.transpose(ps_hot[u % 2][:, k * P:(k + 1) * P], onehot[:, u, k, :], ident[:, :])
                    mm.then_inc(s_hot_turned, 1)

                def products(i, u):
                    g = i * UNROLL + u
                    pe.wait_ge(s_edge_cols, g + 1)
                    pe.wait_ge(s_hot_cols, g + 1)
                    pe.wait_ge(s_b_win[u], (i + 1) * 16)
                    if past(g, 2):
                        pe.wait_ge(s_z, g - 1)
                    for k in range(SUB):
                        to = ps_pre[u % 2][:, k * H:(k + 1) * H]
                        pe.matmul(to, edge_cols[:, u % 2, k * P:(k + 1) * P], w_c[:, :], start=True, stop=False)
                        mm = pe.matmul(to, onehot_cols[:, u % 2, k * P:(k + 1) * P], b_win[:, u, :],
                                       start=False, stop=True)
                    mm.then_inc(s_pre, 1)

                def sums(i, u):
                    g = i * UNROLL + u
                    pe.wait_ge(s_msg, g + 1)
                    if past(g, 2):
                        pe.wait_ge(s_added, g - 1)
                    for k in range(SUB):
                        mm = pe.matmul(ps_sums[u % 2], msg[:, u % 2, k, :], onehot[:, u, k, 0:WIN],
                                       start=(k == 0), stop=(k == SUB - 1))
                    mm.then_inc(s_sum, 1)

                def turn_early(r):
                    pe.wait_ge(s_e_norm, r + 1)
                    pe.wait_ge(s_added, r * UNROLL + 1)
                    pe.transpose(ps_early, e_norm[:, :], ident[:, :]).then_inc(s_e_turned, 1)

                def early_product(r):
                    pe.wait_ge(s_e_cols, r + 1)
                    pe.wait_ge(s_added, r * UNROLL + 3)
                    pe.matmul(ps_early_a, e_cols[:, :], w_a[:, :], start=True, stop=True).then_inc(s_e_a, 1)

                def round_(i, groups=UNROLL, early=False, early_before=False):
                    last = groups < UNROLL
                    for u in range(groups):
                        if not (last and u == groups - 1):
                            turn(*after(i, u, 1))
                        products(i, u)
                        if u == 0 and past(i, 1):
                            if past(i, 3):
                                pe.wait_ge(s_total, i - 2)
                            table_b_block(i - 1)
                        if u == 2:
                            if past(i, 1):
                                pe.wait_ge(s_added, i * UNROLL)
                            if past(i, 2):
                                turn_total(i - 2)
                            if not last:
                                turn_hb(i)
                        if u == 1 and early_before:
                            pe.wait_ge(s_e_rows, i)
                        if u == 3 and early:
                            pe.wait_ge(s_e_cols, i + 1)
                        if past(i * UNROLL + u, 1):
                            sums(*before(i, u))
                        if u == 0 and early_before:
                            early_product(i - 1)
                        if u == 2 and early:
                            turn_early(i)

                turn(0, 0)
                round_(0, early=True)
                round_(1, early=True, early_before=True)
                round_(2, early=True, early_before=True)
                with pe.Fori(3, EARLY_ROWS) as i:
                    round_(i, early=True, early_before=True)
                round_(EARLY_ROWS, early_before=True)
                with pe.Fori(EARLY_ROWS + 1, ROUNDS - 1) as i:
                    round_(i)
                round_(ROUNDS - 1, LEFT)
                sums(ROUNDS - 1, LEFT - 1)
                turn_total(BLOCKS - 2)
                turn_total(BLOCKS - 1, 1)
            with pe.Else():
                turn_hb(0)
                table_b_block(0)
                with pe.Fori(1, ROUNDS - 1) as j:
                    turn_hb(j)
                    table_b_block(j)
                with pe.Fori(0, GROUPS) as g:
                    pe.wait_ge(g_edges, (g + 1) * 16)
                    for k in range(SUB):
                        mm = pe.transpose(ps_edge[0][:, k * P:(k + 1) * P],
                                          edges[:, 0, k * H:(k + 1) * H], ident[:, :])
                    mm.then_inc(g_turned, 1)
                    pe.wait_ge(g_cols, g + 1)
                    for k in range(SUB):
                        mm = pe.matmul(ps_pre[0][:, k * H:(k + 1) * H], edge_cols[:, 0, k * P:(k + 1) * P],
                                       w_c[:, :], start=True, stop=True)
                    mm.then_inc(g_pre, 1)
                    with pe.Fori(0, WIDES) as w:
                        pe.wait_ge(g_msg, g + 1)
                        pe.wait_ge(g_added, g * WIDES + w + 1)
                        pe.wait_ge(g_hot, g * WIDES + w + 1)
                        for k in range(SUB):
                            mm = pe.matmul(ps_sum[:, :], msg[:, 0, k, :], onehot[:, k, :, :],
                                           start=(k == 0), stop=(k == SUB - 1))
                        mm.then_inc(g_sum, 1)
                turn_total(0)
                with pe.Fori(1, BLOCKS) as b:
                    turn_total(b)

        @block.scalar
        def _(act):
            act.wait_ge(s_const, 5)

            def deviate_chunk(c):
                act.wait_ge(s_var, c + 1)
                if past(c, 1):
                    act.wait_ge(s_scale, c)
                act.activation(deviation[:, :], four_var[:, :], ACT.Sqrt, bias=eps[:, 0:1], scale=0.25
                               ).then_inc(s_dev, 1)

            def h_columns(c, par):
                act.wait_ge(s_turned, c + 1)
                if past(c, 2):
                    act.wait_ge(s_tab, c - 1)
                act.activation(h_cols[:, par, 0:4, :].rearrange("p b n -> p (b n)"), ps_turn[par][0][:, :], ACT.Relu)
                act.activation(h_cols[:, par, 4:CHUNK, :].rearrange("p b n -> p (b n)"),
                               ps_turn[par][1][:, 0:(CHUNK - 4) * P], ACT.Relu).then_inc(s_h_cols, 1)

            def keep_a(c, par, half):
                act.wait_ge(s_tab, c + 1)
                if isinstance(c, int) and c == CHUNKS - 1:
                    act.wait_ge(s_turned, CHUNKS - 1)
                elif past(half, 1):
                    act.wait_ge(s_a_stored[par], half * 16)
                act.wait_ge(s_scale, c + 1)
                for k in range(4 if isinstance(c, int) and c >= CHUNKS - SHARED else 0, CHUNK):
                    ins = act.activation(a_tile(c, par)[:, k, :], ps_tab[par][k // 4][:, (k % 4) * H:(k % 4 + 1) * H],
                                         ACT.Copy, scale=scale_all[:, bass.ds(first_block(c) + k, 1)])
                ins.then_inc(s_a_kept[1], 1)

            def cast_ids(a, first):
                act.wait_ge(s_ids[a], ID_LOADS * 16)
                act.activation(ids_f[0:ROWS, a, first:, :], ids_i[0:ROWS, a, first:, :], ACT.Copy
                               ).then_inc(s_cast[a], 1)

            def keep_ids(a, ids, at, quads):
                for q in quads:
                    act.wait_ge(s_ids_turned, at + q + 1)
                    act.activation(ids[:, q * ROWS:(q + 1) * ROWS, :].rearrange("p r k -> p k r"),
                                   ps_ids[a][q][:, 0:SUB * ROWS].rearrange("p (k r) -> p k r", k=SUB),
                                   ACT.Copy).then_inc(s_ids_kept, 1)

            act.activation(o_dev[:, 0:1], eps[:, :], ACT.Sqrt)
            deviate_chunk(0)
            h_columns(0, 0)
            cast_ids(1, 0)
            for c in range(1, 4):
                deviate_chunk(c)
                h_columns(c, c % 2)
                if c >= 2:
                    keep_a(c - 2, c % 2, 0)
            with act.Fori(2, CHUNKS // 2 - 1) as pair:
                for par in range(2):
                    c = pair * 2 + par
                    deviate_chunk(c)
                    h_columns(c, par)
                    keep_a(c - 2, par, pair - 1)
            for c in range(CHUNKS - 2, CHUNKS):
                deviate_chunk(c)
                h_columns(c, c % 2)
                keep_a(c - 2, c % 2, c // 2 - 1)
            for c in range(CHUNKS - 2, CHUNKS):
                keep_a(c, c % 2, c // 2)
            act.wait_ge(s_b_first, 1)
            for k in range(AHEAD):
                ins = act.activation(b_first[:, k, :], ps_first[k // 4][:, (k % 4) * H:(k % 4 + 1) * H],
                                     ACT.Copy, scale=scale_all[:, k:k + 1])
            ins.then_inc(s_b_first_kept, 1)
            keep_ids(0, src_f, 0, range(1))
            cast_ids(0, 2)
            keep_ids(0, src_f, 0, range(1, QUADS))
            act.wait_ge(s_b_first_kept, 2)
            act.dma_start(table_b[0:AHEAD * P, :].rearrange("(b p) f -> p b f", p=P), b_first[:, :, :]
                          ).then_inc(s_b_stored, 16)
            keep_ids(1, dst_f, QUADS, range(QUADS))

            act.wait_ge(s_planned, 1)
            crooked = act.value_load(flag[0:1, 0:1], min_val=0, max_val=ID_ROWS)

            act.wait_ge(s_norm, 1)

            def h_of(rows, b):
                return act.activation(rows, x_block(b), ACT.Relu, bias=shift_all[:, bass.ds(b, 1)],
                                      scale=scale_all[:, bass.ds(b, 1)])

            def h_once_more(b, place=0):
                if place == 0 and past(b, 1):
                    act.wait_ge(s_total, b)
                h_of(h_again[:, place, :], b).then_inc(s_h_again, 1)

            def stage(b, place=0):
                if place == 0 and past(b, 1):
                    act.wait_ge(s_fin_turned, b)
                act.activation(staged[:, place, :], aggr[:, bass.ds(b * P, P)], ACT.Copy).then_inc(s_staged, 1)

            def deviate(b, place=0):
                act.wait_ge(s_o_moments, b + 1)
                if place == 0 and past(b, 1):
                    act.wait_ge(s_o_scale, b)
                act.activation(o_dev[:, place:place + 1], o_moments[:, place, 1:2], ACT.Sqrt, bias=eps[:, 0:1]
                               ).then_inc(s_o_dev, 1)

            def h_ahead(j):
                if past(j, 1):
                    act.wait_ge(s_hb_turned, j)
                h_of(hb_rows[:, :], j + AHEAD).then_inc(s_hb, 1)

            def store_b(j):
                act.wait_ge(s_b_kept, j + 1)
                act.dma_start(table_b[bass.ds((j + AHEAD) * P, P), :], b_rows[:, :]).then_inc(s_b_stored, 16)

            with act.If(crooked < 1):
                def columns(i, u):
                    g = i * UNROLL + u
                    act.wait_ge(s_edge_turned, g + 1)
                    if past(g, 2):
                        act.wait_ge(s_pre, g - 1)
                    act.activation(edge_cols[:, u % 2, :], ps_edge[u % 2][:, :], ACT.Copy).then_inc(s_edge_cols, 1)
                    act.wait_ge(s_hot_turned, g + 1)
                    act.activation(onehot_cols[:, u % 2, :], ps_hot[u % 2][:, :], ACT.Copy).then_inc(s_hot_cols, 1)

                def relu(i, u):
                    act.wait_ge(s_z, i * UNROLL + u + 1)
                    act.activation(msg[:, u % 2, :, :], msg[:, u % 2, :, :], ACT.Relu).then_inc(s_msg, 1)

                def early_deviation(r):
                    act.wait_ge(s_e_moments, r + 1)
                    if past(r, 1):
                        act.wait_ge(s_e_scale, r)
                    act.activation(e_dev[:, :], e_moments[:, 1:2], ACT.Sqrt, bias=eps[:, 0:1]).then_inc(s_e_dev, 1)

                def early_columns(r):
                    act.wait_ge(s_e_turned, r + 1)
                    if past(r, 1):
                        act.wait_ge(s_e_a, r)
                    act.activation(e_cols[:, :], ps_early, ACT.Relu).then_inc(s_e_cols, 1)

                def keep_early(r):
                    act.wait_ge(s_e_a, r + 1)
                    if past(r, 1):
                        act.wait_ge(s_e_stored, r * 16)
                    act.activation(e_rows[:, :], ps_early_a, ACT.Copy).then_inc(s_e_rows, 1)

                def store_early(r):
                    act.wait_ge(s_e_rows, r + 1)
                    act.dma_start(table_early[bass.ds(r * P, P), :], e_rows[:, :]).then_inc(s_e_stored, 16)

                def round_(i, groups=UNROLL, early=False, early_before=False):
                    last = groups < UNROLL
                    for u in range(groups):
                        if not (last and u == groups - 1):
                            columns(*after(i, u, 1))
                        if u == 3 and past(i, 2):
                            deviate(i - 2)
                        if u == 3 and early:
                            early_columns(i)
                        if u == 1 and early_before:
                            keep_early(i - 1)
                        relu(i, u)
                        if u == 1 and early:
                            early_deviation(i)
                        if u == 2 and early_before:
                            store_early(i - 1)
                        if u == 1:
                            if past(i, 2):
                                act.wait_ge(s_added, i * UNROLL)
                                stage(i - 2)
                                h_once_more(i - 2)
                            if not last:
                                h_ahead(i)
                                if past(i, 1):
                                    store_b(i - 1)

                columns(0, 0)
                for i in range(3):
                    round_(i, early=True, early_before=i > 0)
                with act.Fori(3, EARLY_ROWS) as i:
                    round_(i, early=True, early_before=True)
                round_(EARLY_ROWS, early_before=True)
                with act.Fori(EARLY_ROWS + 1, ROUNDS - 1) as i:
                    round_(i)
                round_(ROUNDS - 1, LEFT)
                deviate(ROUNDS - 3)
                h_once_more(BLOCKS - 2)
                h_once_more(BLOCKS - 1, 1)
                act.wait_ge(s_added, GROUPS)
                stage(BLOCKS - 2)
                stage(BLOCKS - 1, 1)
                deviate(BLOCKS - 2)
                deviate(BLOCKS - 1, 1)
            with act.Else():
                h_ahead(0)
                store_b(0)
                with act.Fori(1, ROUNDS - 1) as j:
                    h_ahead(j)
                    store_b(j)
                with act.Fori(0, GROUPS) as g:
                    act.wait_ge(g_turned, g + 1)
                    act.activation(edge_cols[:, 0, :], ps_edge[0][:, :], ACT.Copy).then_inc(g_cols, 1)
                    act.wait_ge(g_z2, g + 1)
                    act.activation(msg[:, 0, :, :], msg[:, 0, :, :], ACT.Relu).then_inc(g_msg, 1)
                act.wait_ge(g_added, GROUPS * WIDES + 1)
                stage(0)
                h_once_more(0)
                deviate(0)
                with act.Fori(1, BLOCKS) as b:
                    stage(b)
                    h_once_more(b)
                    deviate(b)

        @block.vector
        def _(dve):
            def moments(c, par, half):
                loads = 2 if isinstance(c, int) and c == CHUNKS - 2 else 1
                dve.wait_ge(s_x[par], (half + loads) * 16)
                for k in range(CHUNK):
                    ins = dve.bn_stats(halves[:, k, :], x_block(first_block(c) + k))
                ins.then_inc(s_vec, 1)

            def means(c):
                dve.wait_ge(s_vec, c * 3 + 2)
                dve.tensor_scalar(mean_all[:, bass.ds(first_block(c), CHUNK)], pair_sum[:, :, 0], 0.5, None,
                                  ALU.mult)
                dve.tensor_tensor(gap_sq[:, :], pair_gap[:, :], pair_gap[:, :], ALU.mult).then_inc(s_vec, 1)

            def sums(c):
                dve.wait_ge(s_vec, c * 3 + 1)
                if past(c, 1):
                    dve.wait_ge(s_var, c)
                dve.tensor_tensor(pair_sum[:, :, :], halves[:, :, 1:3], halves[:, :, 4:6], ALU.add)
                dve.tensor_tensor(pair_gap[:, :], halves[:, :, 1], halves[:, :, 4], ALU.subtract).then_inc(s_vec, 1)

            def centre(c, par):
                blocks = bass.ds(first_block(c), CHUNK)
                dve.wait_ge(s_vec, c * 3 + 3)
                if past(c, 1):
                    dve.wait_ge(s_dev, c)
                dve.scalar_tensor_tensor(out=four_var[:, :], in0=pair_sum[:, :, 1], scalar=4.0 / H,
                                         in1=gap_sq[:, :], op0=ALU.mult, op1=ALU.add).then_inc(s_var, 1)
                if past(c, 2):
                    dve.wait_ge(s_turned, c - 1)
                dve.tensor_tensor(centred[:, par, :, :], x_all[:, blocks, :],
                                  mean_all[:, blocks].unsqueeze(2).to_broadcast([P, CHUNK, H]), ALU.subtract
                                  ).then_inc(s_centred, 1)

            def scale(c):
                dve.wait_ge(s_dev, c + 1)
                dve.reciprocal(scale_all[:, bass.ds(first_block(c), CHUNK)], deviation[:, :]).then_inc(s_scale, 1)

            def keep_a(c, par):
                dve.wait_ge(s_scale, c + 1)
                dve.wait_ge(s_tab, c + 1)
                if c == CHUNKS - 1:
                    dve.wait_ge(s_turned, CHUNKS - 1)
                else:
                    dve.wait_ge(s_a_stored[par], (c // 2) * 16)
                dve.tensor_tensor(a_tile(c, par)[:, 0:4, :], ps_tab[par][0][:, :].rearrange("p (b f) -> p b f", b=4),
                                  scale_all[:, bass.ds(first_block(c), 4)].unsqueeze(2).to_broadcast([P, 4, H]),
                                  ALU.mult).then_inc(s_a_kept[0], 1)

            def step(c, par, half):
                moments(c + 2, par, half)
                centre(c + 1, 1 - par)
                sums(c + 2)
                scale(c)
                means(c + 2)

            def pick(i, u):
                dve.tensor_copy(picks[:, u, :], src_f[:, bass.ds(i * UNROLL + u, 1), :].rearrange("p o k -> p (o k)")
                                ).then_inc(s_picks, 1)

            def extreme(to, q, op):
                return dve.tensor_reduce(to[0:ROWS, q:q + 1], ids_f[0:ROWS, 1, q, :], AX.X, op)

            dve.memset(scale_all[:, BLOCKS:ALL_BLOCKS], 0.0)
            dve.memset(shift_all[:, BLOCKS:ALL_BLOCKS], 0.0)
            dve.memset(zeros[:, :], 0.0)
            dve.memset(b_win[:, :, :], 0.0)
            dve.memset(onehot[:, :, :, :], 0.0).then_inc(s_zero, 1)
            for c in range(2):
                moments(c, c, 0)
                sums(c)
                means(c)
                if c == 0:
                    centre(c, c)
            for c in range(4):
                step(c, c % 2, c // 2 + 1)
            with dve.Fori(2, CHUNKS // 2 - 2) as pair:
                for par in range(2):
                    step(pair * 2 + par, par, pair + 1)
            for c in range(CHUNKS - 4, CHUNKS - 2):
                step(c, c % 2, c // 2 + 1)
            centre(CHUNKS - 1, 1)
            dve.wait_ge(s_cast[1], 1)
            scale(CHUNKS - 2)
            for q in range(QUADS):
                ins = extreme(lowest, q, ALU.min)
            ins.then_inc(s_range, 1)
            keep_a(CHUNKS - 3, 1)
            scale(CHUNKS - 1)
            for q in range(2):
                extreme(highest, q, ALU.max)
            keep_a(CHUNKS - 2, 0)
            keep_a(CHUNKS - 1, 1)
            for q in range(2, QUADS):
                ins = extreme(highest, q, ALU.max)
            ins.then_inc(s_range, 1)
            dve.wait_ge(s_const, 5)
            dve.wait_ge(s_range, 2)
            dve.tensor_tensor(highest[0:ROWS, :], highest[0:ROWS, :], lowest[0:ROWS, :], ALU.subtract
                              ).then_inc(s_range, 1)
            dve.tensor_tensor(even[0:ROWS, :], lowest[0:ROWS, :], even[0:ROWS, :], ALU.subtract
                              ).then_inc(s_range, 1)
            dve.wait_ge(s_range, 4)
            dve.tensor_scalar(highest[0:ROWS, :], highest[0:ROWS, :], float(WIN), None, ALU.is_ge
                              ).then_inc(s_range, 1)
            dve.tensor_tensor(even[0:ROWS, :], even[0:ROWS, :], even[0:ROWS, :], ALU.mult).then_inc(s_range, 1)
            dve.wait_ge(s_range, 6)
            dve.scalar_tensor_tensor(out=bad[0:ROWS, :], in0=even[0:ROWS, :], scalar=float(LEAD * LEAD),
                                     in1=highest[0:ROWS, :], op0=ALU.is_gt, op1=ALU.max).then_inc(s_bad, 1)
            dve.scalar_tensor_tensor(out=shift_all[:, 0:BLOCKS], in0=mean_all[:, :], scalar=-1.0,
                                     in1=scale_all[:, 0:BLOCKS], op0=ALU.mult, op1=ALU.mult).then_inc(s_norm, 1)
            dve.wait_ge(s_ids_kept, 1)
            for u in range(UNROLL):
                pick(0, u)
            dve.wait_ge(s_plan, 1)
            dve.tensor_copy(flag[:, :], ps_bad).then_inc(s_planned, 1)
            dve.tensor_copy(base_i[:, :], ps_base[0:1, 0:ID_ROWS]).then_inc(s_planned, 1)
            dve.tensor_copy(base_all[:, :], ps_base[:, 0:ID_ROWS]).then_inc(s_planned, 1)

            dve.wait_ge(s_planned, 3)
            crooked = dve.value_load(flag[0:1, 0:1], min_val=0, max_val=ID_ROWS)
            dve.wait_ge(s_zero, 1)
            dve.wait_ge(s_pad, 2)
            dve.wait_ge(s_early_raw, EARLY_ROWS * 16)

            def mask():
                dve.wait_ge(s_ids_kept, 2 * QUADS)
                dve.memset(dst_f[0:TAIL_DONE, FULL_GROUPS, :], -1.0).then_inc(s_rel, 1)
                dve.wait_ge(s_rel, 1)

            def hb_columns(j):
                dve.wait_ge(s_hb_turned, j + 1)
                if past(j, 1):
                    dve.wait_ge(s_b_tab, j)
                dve.tensor_copy(hb_cols[:, :], ps_hb).then_inc(s_hb_cols, 1)

            def keep_b(j):
                dve.wait_ge(s_b_tab, j + 1)
                dve.wait_ge(s_b_stored, (j + 1) * 16)
                dve.tensor_tensor(b_rows[:, :], ps_b, b1_all[:, :], ALU.add).then_inc(s_b_kept, 1)

            def add_beta(b, place=0):
                if place == 0 and past(b, 1):
                    dve.wait_ge(s_out, b)
                dve.tensor_tensor(x_beta[:, place, :], x_block(b), beta_all[:, :], ALU.add).then_inc(s_x_beta, 1)

            def add_h(b, place=0):
                dve.wait_ge(s_fin_turned, b + 1)
                dve.wait_ge(s_h_again, b + 1)
                if place == 0 and past(b, 1):
                    dve.wait_ge(s_scaled, b)
                    dve.wait_ge(s_out, b)
                dve.tensor_tensor(total[:, place, :], ps_total[place], h_again[:, place, :], ALU.add
                                  ).then_inc(s_total, 1)
                dve.wait_ge(s_total, b + 1)
                dve.bn_stats(o_halves[:, place, :], total[:, place, :]).then_inc(s_o_halves, 1)
                dve.wait_ge(s_o_halves, b + 1)
                dve.sem_inc(s_gate_dve, 1)
                dve.bn_aggr(o_moments[:, place, :], o_halves[:, place, :]).then_inc(s_o_moments, 1)
                dve.wait_ge(s_o_moments, b + 1)
                dve.scalar_tensor_tensor(out=scaled[:, place, :], in0=total[:, place, :],
                                         scalar=o_moments[:, place, 0:1], in1=gamma_all[:, :],
                                         op0=ALU.subtract, op1=ALU.mult).then_inc(s_scaled, 1)

            def finish(b, place=0):
                dve.wait_ge(s_o_dev, b + 1)
                dve.reciprocal(o_scale[:, place:place + 1], o_dev[:, place:place + 1]).then_inc(s_o_scale, 1)
                if place == 0 and past(b, 1):
                    dve.wait_ge(s_out_stored, b * 16)
                dve.wait_ge(s_scaled, b + 1)
                dve.wait_ge(s_x_beta, b + 1)
                dve.wait_ge(s_o_scale, b + 1)
                dve.scalar_tensor_tensor(out=out_rows[:, place, :], in0=scaled[:, place, :],
                                         scalar=o_scale[:, place:place + 1], in1=x_beta[:, place, :],
                                         op0=ALU.mult, op1=ALU.add).then_inc(s_out, 1)

            with dve.If(crooked < 1):
                def one_hot(i, u):
                    if past(i, 1):
                        dve.wait_ge(s_sum, (i - 1) * UNROLL + u + 1)
                    dve.tensor_tensor(
                        onehot[:, u, :, 0:WIN],
                        dst_f[:, bass.ds(i * UNROLL + u, 1), :].rearrange("p o k -> p (o k)").unsqueeze(2)
                        .to_broadcast([P, SUB, WIN]),
                        count[:, 0:WIN].unsqueeze(1).to_broadcast([P, SUB, WIN]),
                        ALU.is_equal).then_inc(s_hot, 1)

                def add_a(i, u, turn, loaded):
                    g = i * UNROLL + u
                    dve.wait_ge(s_pre, g + 1)
                    if loaded is not None:
                        dve.wait_ge(s_early_loaded, loaded * 16)
                    else:
                        for k in range(SUB):
                            dve.wait_ge(s_a_rows[u][k], (turn if u == UNROLL - 1 else i + 1) * 16)
                    if past(g, 2):
                        dve.wait_ge(s_sum, g - 1)
                    dve.tensor_tensor(msg[:, u % 2, :, :].rearrange("p k f -> p (k f)"), ps_pre[u % 2][:, :],
                                      a_rows[:, u, :, :].rearrange("p k f -> p (k f)"), ALU.add).then_inc(s_z, 1)

                def base_of(g):
                    return dve.value_load(base_i[0:1, bass.ds(g, 1)], min_val=0, max_val=N - 1)

                def add_sums(i, u, base=None):
                    g = i * UNROLL + u
                    if base is None:
                        base = base_of(g)
                    dve.wait_ge(s_sum, g + 1)
                    if past(g, 1):
                        dve.wait_ge(s_added, g)
                    at = aggr[:, bass.ds(base, WIN)]
                    dve.tensor_tensor(at, ps_sums[u % 2], at, ALU.add).then_inc(s_added, 1)

                def early_moments(r):
                    raw = aggr[:, bass.ds((r + EARLY_AT) * P, P)]
                    dve.bn_stats(e_halves[:, :], raw).then_inc(s_e_halves, 1)
                    dve.wait_ge(s_e_halves, r + 1)
                    dve.sem_inc(s_gate_dve, 1)
                    dve.bn_aggr(e_moments[:, :], e_halves[:, :]).then_inc(s_e_moments, 1)

                def early_scale(r):
                    dve.wait_ge(s_e_dev, r + 1)
                    dve.reciprocal(e_scale[:, :], e_dev[:, :]).then_inc(s_e_scale, 1)

                def early_normalise(r):
                    raw = aggr[:, bass.ds((r + EARLY_AT) * P, P)]
                    dve.wait_ge(s_e_scale, r + 1)
                    if past(r, 1):
                        dve.wait_ge(s_e_turned, r)
                    dve.tensor_scalar(e_norm[:, :], raw, e_moments[:, 0:1], e_scale[:, 0:1],
                                      ALU.subtract, ALU.mult).then_inc(s_e_norm, 1)

                def clear(j):
                    dve.tensor_copy(aggr[:, bass.ds((j + AHEAD) * P, P)], zeros[:, :])

                def round_(i, turn, groups=UNROLL, early=False, loaded=None):
                    last = groups < UNROLL
                    for u in range(groups):
                        if not (last and u + 2 >= groups):
                            one_hot(*after(i, u, 2))
                        if u == 0 and early:
                            early_moments(i)
                        if u == 2 and early:
                            early_scale(i)
                        add_a(i, u, turn, loaded if u == UNROLL - 1 else None)
                        if not last and not (isinstance(i, int) and i == ROUNDS - 2 and u >= LEFT):
                            pick(i + 1, u)
                        if past(i * UNROLL + u, 1):
                            add_sums(*before(i, u))
                        if u == 2 and early:
                            early_normalise(i)
                        if u == 0 and past(i, 1):
                            clear(i - 1)
                            keep_b(i - 1)
                        if u == 2:
                            if past(i, 2):
                                add_beta(i - 2)
                                add_h(i - 2)
                            if not last:
                                hb_columns(i)
                        if u == 3 and past(i, 2):
                            finish(i - 2)

                mask()
                dve.tensor_tensor(dst_f[:, :, :], dst_f[:, :, :],
                                  base_all[:, :].unsqueeze(2).to_broadcast([P, ID_ROWS, SUB]),
                                  ALU.subtract).then_inc(s_rel, 1)
                dve.memset(aggr[:, 0:AHEAD * P], 0.0)
                dve.wait_ge(s_rel, 2)
                one_hot(0, 0)
                one_hot(0, 1)
                def rounds(s, early):
                    with dve.Fori(0, EARLY - 1) as j:
                        round_(s * EARLY + j, s * (EARLY - 1) + j + 1, early=early)
                    round_(s * EARLY + EARLY - 1, None, early=early, loaded=s + 1)

                for i in range(3):
                    round_(i, i + 1, early=True)
                with dve.Fori(3, EARLY - 1) as i:
                    round_(i, i + 1, early=True)
                round_(EARLY - 1, None, early=True, loaded=1)
                with dve.Fori(1, EARLY_ROWS // EARLY) as s:
                    rounds(s, True)
                with dve.Fori(EARLY_ROWS // EARLY, EARLY_GROUPS) as s:
                    rounds(s, False)
                round_(ROUNDS - 2, ROUNDS - 1 - EARLY_GROUPS)
                round_(ROUNDS - 1, None, LEFT)
                base = base_of(GROUPS - 1)
                add_beta(BLOCKS - 1, 1)
                finish(ROUNDS - 3)
                add_beta(BLOCKS - 2)
                add_sums(ROUNDS - 1, LEFT - 1, base)
                add_h(BLOCKS - 2)
                add_h(BLOCKS - 1, 1)
                finish(BLOCKS - 2)
                finish(BLOCKS - 1, 1)
            with dve.Else():
                mask()
                dve.memset(aggr[:, :], 0.0).then_inc(g_added, 1)
                dve.wait_ge(g_added, 1)
                hb_columns(0)
                keep_b(0)
                with dve.Fori(1, ROUNDS - 1) as j:
                    hb_columns(j)
                    keep_b(j)
                with dve.Fori(0, GROUPS) as g:
                    senders = src_f[:, bass.ds(g, 1), :].rearrange("p o k -> p (o k)")
                    receivers = dst_f[:, bass.ds(g, 1), :].rearrange("p o k -> p (o k)")
                    dve.tensor_copy(picks[:, 0, :], senders).then_inc(g_picks, 1)
                    dve.tensor_scalar(picks[:, 1, :], receivers, 0.0, None, ALU.max).then_inc(g_picks, 1)
                    dve.wait_ge(g_pre, g + 1)
                    for k in range(2 * SUB):
                        dve.wait_ge(g_rows[k], (g + 1) * 16)
                    z = msg[:, 0, :, :].rearrange("p k f -> p (k f)")
                    dve.tensor_tensor(z, ps_pre[0][:, :], a_rows[:, 0, :, :].rearrange("p k f -> p (k f)"),
                                      ALU.add).then_inc(g_z, 1)
                    dve.wait_ge(g_z, g + 1)
                    dve.tensor_tensor(z, z, a_rows[:, 1, :, :].rearrange("p k f -> p (k f)"), ALU.add
                                      ).then_inc(g_z2, 1)
                    with dve.Fori(0, WIDES) as w:
                        for k in range(SUB):
                            ins = dve.tensor_scalar(onehot[:, k, :, :].rearrange("p k n -> p (k n)"), count[:, :],
                                                    receivers[:, k:k + 1], None, ALU.is_equal)
                        ins.then_inc(g_hot, 1)
                        dve.wait_ge(g_hot, g * WIDES + w + 1)
                        dve.tensor_scalar(receivers, receivers, -float(WIDE), None, ALU.add).then_inc(g_rel, 1)
                        dve.wait_ge(g_sum, g * WIDES + w + 1)
                        at = aggr[:, bass.ds(w * WIDE, WIDE)]
                        dve.tensor_tensor(at, ps_sum[:, :], at, ALU.add).then_inc(g_added, 1)
                        dve.wait_ge(g_added, g * WIDES + w + 2)
                        dve.wait_ge(g_rel, g * WIDES + w + 1)
                add_beta(0)
                add_h(0)
                finish(0)
                with dve.Fori(1, BLOCKS) as b:
                    add_beta(b)
                    add_h(b)
                    finish(b)


_INS = ["x", "src", "dst", "edge_attr_128", "L0_gnn_W1", "L0_gnn_b1", "L0_gnn_ln_gamma", "L0_gnn_ln_beta"]


def kernel(**inputs):
    import numpy as _np
    import concourse.bacc as _bacc
    from concourse import mybir as _mybir
    from concourse.bass_utils import run_bass_kernel_spmd as _run

    nc = _bacc.Bacc("TRN2", target_bir_lowering=False, num_devices=1)
    arrays, args = {}, []
    for name in _INS:
        a = _np.ascontiguousarray(inputs[name])
        arrays[f"in_{name}"] = a
        args.append(nc.dram_tensor(f"in_{name}", a.shape, _mybir.dt.from_np(a.dtype), kind="ExternalInput").ap())
    shape = inputs["x"].shape
    args.append(nc.dram_tensor("out_0", shape, _mybir.dt.float32, kind="ExternalOutput").ap())
    build(nc, *args)
    r = _run(nc, [arrays], core_ids=[0])
    return r.results[0]["out_0"]
```
